# Optimizing a Trainium2 kernel written in Bass

```python
import numpy as np
import jax
import jax.numpy as jnp

def _softmax(x, axis=-1):
    return jax.nn.softmax(x, axis=axis)

def _gelu(x):
    return jax.nn.gelu(x, approximate=True)

def _silu(x):
    return jax.nn.silu(x)

def _sigmoid(x):
    return jax.nn.sigmoid(x)

def _layernorm(x, axis=-1, eps=1e-05):
    m = jnp.mean(x, axis=axis, keepdims=True)
    v = jnp.var(x, axis=axis, keepdims=True)
    return (x - m) / jnp.sqrt(v + eps)

def _scatter_add(tgt, idx, src, axis=0):
    return tgt.at[idx].add(src)

def _segment_sum(src, seg, n):
    return jax.ops.segment_sum(src, seg, n)
kernel_name = 'mk_seq_preln_d1_jaxref_r4_2909f6'

def setup_inputs(seed: int=0):
    np.random.seed(seed)
    _w = jnp.asarray

    def _L0_attn_setup():
        import jax, jax.numpy as jnp
        import numpy as np
        B, S, D, H = (2, 512, 256, 16)
        HD = D // H
        key = jax.random.key(seed)
        k0, k1, k2 = jax.random.split(key, 3)
        return {'x': jax.random.normal(k0, (B, S, D), jnp.float32), 'qkv_w': jax.random.normal(k1, (D, 3 * D), jnp.float32) / np.sqrt(D).astype(np.float32), 'qkv_b': jnp.zeros((3 * D,), jnp.float32), 'out_w': jax.random.normal(k2, (D, D), jnp.float32) / np.sqrt(D).astype(np.float32), 'out_b': jnp.zeros((D,), jnp.float32)}
    _L0_attn_in = _L0_attn_setup()

    def _L0_ffn_setup():
        import jax, jax.numpy as jnp
        import numpy as np
        B, L, D = (2, 256, 256)
        HID, E, K = (512, 8, 2)
        key = jax.random.key(seed)
        ks = jax.random.split(key, 4)
        std = 0.02
        return {'x': jax.random.normal(ks[0], (B, L, D), dtype=jnp.float32), 'router_scale': jnp.ones((D,), dtype=jnp.float32), 'router_w': jax.random.normal(ks[1], (D, E), dtype=jnp.float32) * std, 'gating_w': jax.random.normal(ks[2], (E, 2, HID, D), dtype=jnp.float32) * std, 'linear_w': jax.random.normal(ks[3], (E, HID, D), dtype=jnp.float32) * std, 'per_expert_scale': jnp.ones((E,), dtype=jnp.float32)}
    _L0_ffn_in = _L0_ffn_setup()
    _d = {'L0_attn_x': _L0_attn_in['x'], 'L0_attn_qkv_w': _L0_attn_in['qkv_w'], 'L0_attn_qkv_b': _L0_attn_in['qkv_b'], 'L0_attn_out_w': _L0_attn_in['out_w'], 'L0_attn_out_b': _L0_attn_in['out_b'], 'L0_ffn_router_scale': _L0_ffn_in['router_scale'], 'L0_ffn_router_w': _L0_ffn_in['router_w'], 'L0_ffn_gating_w': _L0_ffn_in['gating_w'], 'L0_ffn_linear_w': _L0_ffn_in['linear_w'], 'L0_ffn_per_expert_scale': _L0_ffn_in['per_expert_scale']}
    _x0 = _d['L0_attn_x']
    _d['L0_attn_x'] = jax.random.normal(jax.random.fold_in(jax.random.key(seed), 1), (8, 1024, 256), dtype=_x0.dtype)
    del _x0
    return _d

def reference(L0_attn_x, L0_attn_qkv_w, L0_attn_qkv_b, L0_attn_out_w, L0_attn_out_b, L0_ffn_router_scale, L0_ffn_router_w, L0_ffn_gating_w, L0_ffn_linear_w, L0_ffn_per_expert_scale):

    def _L0_attn_ref(x, qkv_w, qkv_b, out_w, out_b):
        import jax, jax.numpy as jnp
        import numpy as np
        B, S, D, H = (2, 512, 256, 16)
        HD = D // H
        b, s, d = x.shape
        h, hd = (H, d // H)
        scale = 1.0 / np.sqrt(hd).astype(np.float32)
        qkv = (x @ qkv_w + qkv_b).reshape(b, s, 3, h, hd)
        q, k, v = (qkv[:, :, 0], qkv[:, :, 1], qkv[:, :, 2])
        logits = jnp.einsum('bqhd,bkhd->bhqk', q, k)
        causal_mask = jnp.triu(jnp.ones((s, s), bool), 1)
        logits = jnp.where(causal_mask, -jnp.inf, logits) * scale
        att = jax.nn.softmax(logits, axis=-1)
        out = jnp.einsum('bhqk,bkhd->bqhd', att, v).reshape(b, s, d)
        return out @ out_w + out_b

    def _L0_ffn_ref(x, router_scale, router_w, gating_w, linear_w, per_expert_scale):
        import jax, jax.numpy as jnp
        import numpy as np
        B, L, D = (2, 256, 256)
        HID, E, K = (512, 8, 2)
        d = x.shape[-1]
        var = jnp.mean(jnp.square(x), axis=-1, keepdims=True)
        r_in = x * jax.lax.rsqrt(var + 1e-06)
        r_in = r_in * jax.lax.rsqrt(jnp.array(d, dtype=r_in.dtype)) * router_scale
        logits = jnp.dot(r_in, router_w).astype(jnp.float32)
        probs = jax.nn.softmax(logits, axis=-1)
        _, top_k_idx = jax.lax.top_k(logits, K)
        indicator = jax.nn.one_hot(top_k_idx, probs.shape[-1], dtype=probs.dtype)
        gate_weights = indicator.sum(axis=-2) * probs
        renorm = jnp.sum(gate_weights, axis=-1, keepdims=True)
        renorm = jnp.where(renorm > 0.0, renorm, 1.0)
        weights = probs / renorm
        top_k_w = jnp.take_along_axis(weights, top_k_idx, axis=-1)
        combine = jnp.einsum('blke,blk->ble', indicator, top_k_w)
        combine = combine * per_expert_scale
        gate0 = jnp.einsum('bld,ehd->bleh', x, gating_w[:, 0])
        gate1 = jnp.einsum('bld,ehd->bleh', x, gating_w[:, 1])
        act = jax.nn.gelu(gate0) * gate1
        out = jnp.einsum('bleh,ehd,ble->bld', act, linear_w, combine)
        return out.astype(x.dtype)
    x = L0_attn_x
    x = x + _L0_attn_ref(_layernorm(x, axis=-1), L0_attn_qkv_w, L0_attn_qkv_b, L0_attn_out_w, L0_attn_out_b)
    x = x + _L0_ffn_ref(_layernorm(x, axis=-1), L0_ffn_router_scale, L0_ffn_router_w, L0_ffn_gating_w, L0_ffn_linear_w, L0_ffn_per_expert_scale)
    return x

_drawn_inputs = setup_inputs


def setup_inputs(seed=0):
    import zlib

    import numpy as np

    out = dict(_drawn_inputs(seed))
    spreads = {'L0_attn_qkv_b': (0.0, 0.1),
     'L0_attn_out_b': (0.0, 0.1),
     'L0_ffn_router_scale': (1.0, 0.6),
     'L0_ffn_per_expert_scale': (1.0, 0.6)}
    factors = {'L0_ffn_router_w': 3.619, 'L0_ffn_gating_w': 3.128, 'L0_ffn_linear_w': 3.125}
    for name, (base, spread) in spreads.items():
        noise = np.random.default_rng([zlib.crc32(name.encode()), seed]).standard_normal(out[name].shape)
        drawn = base * np.exp(spread * noise) if base else spread * noise
        out[name] = jnp.asarray(drawn.astype(out[name].dtype))
    for name, factor in factors.items():
        out[name] = (out[name] * factor).astype(out[name].dtype)
    return out
```

```python
import concourse.bass as bass
from concourse import mybir
from contextlib import ExitStack

F32 = mybir.dt.float32
F32R = mybir.dt.float32r
BF16 = mybir.dt.bfloat16
I32 = mybir.dt.int32
ALU = mybir.AluOpType
ACT = mybir.ActivationFunctionType
AX = mybir.AxisListType
ds = bass.ds

P = 128
HEADS = 16
HD = 16
D = HEADS * HD
ROWS = 64
PRODUCTS = 3 * HD
SCORED = PRODUCTS + 2
E = 8
TOP = 2
MASKED = -1e30
LOWEST = -3e38
RSQRT_MAGIC = 0x5F3759DF
ROW = D + 2


class Chain:

    def __init__(self, engine, sem, per_round, fixed=0):
        self.engine, self.sem, self.per_round, self.n, self.fixed = engine, sem, per_round, 0, fixed
        self.base = fixed

    def begin(self, round_):
        self.base, self.n = round_ * self.per_round + self.fixed, 0

    def link(self, instruction):
        self.n += 1
        instruction.then_inc(self.sem, 1)
        self.engine.wait_ge(self.sem, self.base + self.n)

    def end(self):
        assert self.n == self.per_round, (self.n, self.per_round)


def preln_attention_then_routed_ffn(
    nc: bass.Bass,
    x: bass.AP,
    qkv_w: bass.AP,
    qkv_b: bass.AP,
    out_w: bass.AP,
    out_b: bass.AP,
    router_scale: bass.AP,
    router_w: bass.AP,
    gate_w: bass.AP,
    linear_w: bass.AP,
    expert_scale: bass.AP,
    out: bass.AP,
):
    B, S, _ = x.shape
    HID = linear_w.shape[1]
    T = B * S
    NT = S // P
    HALF = NT // 2
    HC = HID // P
    DC = D // P
    PAIRS = HEADS // 2
    REGION = T + P
    ZEROS = E * REGION
    MT = TOP * T // P + E
    AHEAD = 2
    NOWHERE = 1 << 20
    UNITS = 2 * NT
    CHUNKS = 2 * (HALF + 2 * (NT - HALF))
    ROUNDS = 6
    BR = PAIRS * ROUNDS

    x_rows = x.rearrange("b (t p) d -> b p t d", p=P)
    out_rows = out.rearrange("b (t p) d -> b p t d", p=P)
    x2_dram = nc.dram_tensor("x2_dram", [B, S, D], F32, kind="Internal").ap()
    x2_rows = x2_dram.rearrange("b (t p) d -> b p t d", p=P)
    routed = nc.dram_tensor("routed", [ZEROS + P, ROW], F32, kind="Internal").ap()
    expert_out = nc.dram_tensor("expert_out", [TOP * T, D], F32, kind="Internal").ap()
    expert_rows = expert_out.rearrange("(k b t p) d -> k b p t d", k=TOP, b=B, p=P)

    with ExitStack() as ctx:
        def sb(name, shape, dt=F32):
            return ctx.enter_context(nc.sbuf_tensor(name, shape, dt))

        def sem(name):
            return ctx.enter_context(nc.semaphore(name))

        wg = sb("wg", [P, DC, E, 2 * HID])
        shared = sb("shared", [P, HC * E * D])
        qkv = shared[:, 0:NT * 3 * D].rearrange("p (t n) -> p t n", t=NT)
        attn = shared[:, NT * 3 * D:NT * 4 * D].rearrange("p (t n) -> p t n", t=NT)
        wl = shared[:, :].rearrange("p (c e d) -> p c e d", c=HC, e=E)
        wqkv = sb("wqkv", [P, DC, 3 * D])
        wout = sb("wout", [P, DC, D])
        qkv_bias = sb("qkv_bias", [P, 3 * D])
        out_bias = sb("out_bias", [P, D])
        xin = sb("xin", [P, NT, D])
        xn = sb("xn", [P, 2, D])
        xT = sb("xT", [P, 2, DC, P])
        Qa = [sb(f"Qa{i}", [P, NT, 2, ROWS], F32R) for i in range(2)]
        Ka = [sb(f"Ka{i}", [P, NT, 2, ROWS], F32R) for i in range(2)]
        V = [sb(f"V{i}", [P, NT, 2, 32]) for i in range(2)]
        KT = [sb(f"KT{i}", [P, S], F32R) for i in range(2)]
        QT = sb("QT", [P, S], F32R)
        QTm = sb("QTm", [P, S], F32R)
        probs = sb("probs", [P, 4, S])
        OT = sb("OT", [P, 4 * P])
        xres = sb("xres", [P, NT, D])
        rows = [sb(f"rows{k}", [P, NT, ROW]) for k in range(TOP)]
        ident = sb("ident", [P, P])
        identb = sb("identb", [P, P], BF16)
        mask_qk = sb("mask_qk", [P, P], BF16)
        mask_kq = sb("mask_kq", [P, P], BF16)
        not_before = sb("not_before", [P, P])
        ones = sb("ones", [P, P])
        zero_row = sb("zero_row", [P, ROW])
        maxima = sb("maxima", [P, 2, NT, 2])
        top_score = sb("top_score", [P, 2, NT])
        rden = sb("rden", [P, HALF, 4])
        stats = sb("stats", [P, NT, 6])
        moments = sb("moments", [P, NT, 2])
        var = sb("var", [P, NT])
        rstd = sb("rstd", [P, NT])
        newton = sb("newton", [P, NT])
        scale_raw = sb("scale_raw", [P, DC])
        router_raw = sb("router_raw", [P, DC, E])
        router = sb("router", [P, DC, E])
        escale = sb("escale", [P, E])
        e_index = sb("e_index", [P, E, NT])
        e_start = sb("e_start", [P, E, NT])
        same_expert = sb("same_expert", [P, E, NT])
        token = sb("token", [P, NT])
        running = sb("running", [P, E])
        R = {n: sb("r_" + n, [P, E, NT]) for n in
             ("logits", "left", "pick0", "pick1", "chosen", "count", "slot", "exps", "work", "scale")}
        V1 = {n: sb("v_" + n, [P, NT]) for n in ("best", "index", "sum", "rsum", "gate", "flag", "w", "dest")}
        slot_index = [sb(f"slot_index{k}", [P, NT], I32) for k in range(TOP)]
        tail_f = sb("tail_f", [P, E])
        tail_index = sb("tail_index", [P, E], I32)
        table_row = sb("table_row", [1, MT], I32)
        table_expert = sb("table_expert", [1, MT], I32)
        step_index = sb("step_index", [1, MT])
        tile_start = sb("tile_start", [1, T // P])

        def pb(name, n):
            return ctx.enter_context(nc.psum_tensor(name, [P, n], F32))
        S2 = [pb(f"S2_{i}", 1024) for i in range(2)]
        S1 = [pb(f"S1_{i}", 512) for i in range(2)]
        TB = pb("TB", 512)
        OB = pb("OB", 512)
        round_bank = [TB, S1[0], S1[1]]
        turn_bank = [TB, OB]

        s_wq = sem("weights_in"); s_wg = sem("gate_weights_in"); s_wl = sem("linear_weights_in")
        s_const = sem("constants_made"); s_dconst = sem("vector_constants")
        s_x = sem("x_in"); s_res = sem("residual_in"); s_resb = sem("residual_biased")
        s_xn = sem("xn_ready"); s_turn = sem("turned"); s_turned = sem("turned_copied")
        s_qkvp = sem("qkv_summed"); s_qkv = sem("qkv_ready")
        s_build = sem("qk_rows_built"); s_v = sem("v_built"); s_pool = sem("pool_step")
        s_round = sem("round_turned"); s_rounded = sem("round_copied")
        s_s1 = sem("scores_ready"); s_s1r = sem("scores_reduced"); s_m = sem("maxima_in_rows"); s_mstep = sem("max_step")
        s_s2 = sem("shifted_scores_ready"); s_e = sem("probs_ready"); s_pv = sem("pv_done")
        s_o = sem("o_copied"); s_ot = sem("o_turned"); s_norm = sem("o_normalised"); s_nstep = sem("norm_step")
        s_proj = sem("projected"); s_x2 = sem("x2_ready"); s_h = sem("h_ready"); s_logit = sem("logits_summed")
        s_soft = sem("router_shifted"); s_softed = sem("router_exps")
        s_chosen = sem("chosen_ready"); s_rank = sem("ranks_summed"); s_slot = sem("slots_ready")
        s_scat = sem("rows_scattered"); s_x2out = sem("x2_stored"); s_chain = sem("vector_step")
        s_pool_passed = sem("pool_waits_passed"); s_dve_passed = sem("vector_waits_passed")
        s_tail = sem("tail_ready"); s_tailout = sem("tails_zeroed"); s_table = sem("table_ready")

        LN_STEPS = 3 * 3 + 3
        with nc.Block() as block:

            @block.sync
            def _(sp):
                sp.dma_start(wqkv[:], qkv_w.rearrange("(c p) n -> p c n", p=P)).then_inc(s_wq, 16)
                sp.dma_start(wout[:], out_w.rearrange("(c p) n -> p c n", p=P)).then_inc(s_wq, 16)
                sp.dma_start(qkv_bias[:], qkv_b.partition_broadcast(P)).then_inc(s_wq, 16)
                sp.dma_start(out_bias[:], out_b.partition_broadcast(P)).then_inc(s_wq, 16)
                sp.dma_start(scale_raw[:], router_scale.rearrange("(c p) -> p c", p=P),
                             allow_slow_non_contiguous=True).then_inc(s_wq, 16)
                sp.dma_start(router_raw[:], router_w.rearrange("(c p) e -> p c e", p=P)).then_inc(s_wq, 16)
                sp.dma_start(escale[:], expert_scale.partition_broadcast(P)).then_inc(s_wq, 16)

                def sequence(b, more):
                    if more:
                        sp.wait_ge(s_xn, (b + 1) * NT)
                        sp.dma_start(xin[:], x_rows[b + 1]).then_inc(s_x, 16)
                    sp.wait_ge(s_x2out, b * 16)
                    sp.wait_ge(s_h, b)
                    sp.dma_start(xres[:], x_rows[b]).then_inc(s_res, 16)
                    sp.wait_ge(s_x2, (b + 1) * NT)
                    sp.dma_start(x2_rows[b], xres[:]).then_inc(s_x2out, 16)

                sp.dma_start(xin[:], x_rows[0]).then_inc(s_x, 16)
                if B > 1:
                    with sp.Fori(0, B - 1, 1) as b:
                        sequence(b, True)
                sequence(B - 1, False)
                sp.wait_ge(s_x2out, B * 16)
                sp.wait_ge(s_wg, 16)

            @block.gpsimd
            def _(pool):
                chain = Chain(pool, s_pool, 0)
                link = chain.link
                link(pool.memset(ident[:], 0.0))
                pool.affine_select(out=ident[:], in_=ident[:], compare_op=ALU.not_equal, fill=1.0, base=0,
                                   pattern=[[-1, P]], channel_multiplier=1).then_inc(s_const, 1)
                link(pool.memset(identb[:], 0.0))
                pool.affine_select(out=identb[:], in_=identb[:], compare_op=ALU.not_equal, fill=1.0, base=0,
                                   pattern=[[-1, P]], channel_multiplier=1).then_inc(s_const, 1)
                link(pool.memset(mask_qk[:], 0.0))
                pool.affine_select(out=mask_qk[:], in_=mask_qk[:], compare_op=ALU.is_ge, fill=MASKED, base=0,
                                   pattern=[[-1, P]], channel_multiplier=1).then_inc(s_const, 1)
                link(pool.memset(mask_kq[:], 0.0))
                pool.affine_select(out=mask_kq[:], in_=mask_kq[:], compare_op=ALU.is_ge, fill=MASKED, base=0,
                                   pattern=[[1, P]], channel_multiplier=-1).then_inc(s_const, 1)
                link(pool.memset(not_before[:], 0.0))
                pool.affine_select(out=not_before[:], in_=not_before[:], compare_op=ALU.is_gt, fill=-1.0, base=0,
                                   pattern=[[1, P]], channel_multiplier=-1).then_inc(s_const, 1)
                pool.memset(ones[:], 1.0).then_inc(s_const, 1)
                pool.iota(e_index[:], pattern=[[1, E], [0, NT]], base=0, channel_multiplier=0,
                          allow_small_or_imprecise_dtypes=True).then_inc(s_const, 1)
                pool.iota(token[:], pattern=[[P, NT]], base=0, channel_multiplier=1,
                          allow_small_or_imprecise_dtypes=True).then_inc(s_const, 1)
                pool.memset(zero_row[:], 0.0).then_inc(s_const, 1)
                for i in range(2):
                    pool.memset(V[i][:], 0.0).then_inc(s_const, 1)
                pool.wait_ge(s_const, 11)
                for i in range(2):
                    pool.memset(V[i][:, :, :, HD:HD + 1], 1.0).then_inc(s_const, 1)
                pool.wait_ge(s_dconst, 1)
                pool.dma_start(wg[:], gate_w.rearrange("(c p) e g h -> p c e (g h)", p=P)).then_inc(s_wg, 16)
                pool.wait_ge(s_dconst, 2)
                pool.dma_start(routed[ZEROS:ZEROS + P, :], zero_row[:]).then_inc(s_tailout, 16)
                setup_steps = chain.n

                def hold(semaphore, value):
                    pool.wait_ge(semaphore, value)
                    pool.sem_inc(s_pool_passed, 1)

                def build_qk(g, s, par):
                    for rows_of, at, hi, lo in ((Qa[par], 0, (0, 1), 2), (Ka[par], D, (0, 2), 1)):
                        src = qkv[:, :, ds(at + s * 2 * HD, 2 * HD)].rearrange("p t (j d) -> p t j d", j=2)
                        for n in hi:
                            last = pool.tensor_copy(rows_of[:, :, :, n * HD:(n + 1) * HD], src)
                            last.then_inc(s_pool, 1)
                        hold(s_pool, setup_steps + g * 4 + (2 if at == 0 else 4))
                        last = pool.tensor_tensor(rows_of[:, :, :, lo * HD:(lo + 1) * HD], src,
                                                  rows_of[:, :, :, 0:HD].bitcast(F32), ALU.subtract)
                    last.then_inc(s_build, 1)

                def build_v(s, par):
                    src = qkv[:, :, ds(2 * D + s * 2 * HD, 2 * HD)].rearrange("p t (j d) -> p t j d", j=2)
                    pool.tensor_copy(V[par][:, :, :, 0:HD], src).then_inc(s_v, 1)

                def slot(b, s, par, more, next_v):
                    if more:
                        hold(s_round, b * BR + s * ROUNDS + 6)
                        build_qk(b * PAIRS + s + 2, s + 2, par)
                    if next_v:
                        hold(s_pv, 2 + (b * PAIRS + s) * NT)
                        build_v(s + 1, 1 - par)

                with pool.Fori(0, B, 1) as b:
                    hold(s_qkv, 2 + (b + 1) * NT)
                    build_qk(b * PAIRS, 0, 0)
                    build_v(0, 0)
                    build_qk(b * PAIRS + 1, 1, 1)
                    with pool.Fori(0, PAIRS // 2 - 1, 1) as i:
                        for par in range(2):
                            slot(b, 2 * i + par, par, True, True)
                    slot(b, PAIRS - 2, 0, False, True)
                    hold(s_res, (b + 1) * 16)
                    pool.tensor_tensor(xres[:], xres[:], out_bias[:].unsqueeze(1).to_broadcast([P, NT, D]),
                                       ALU.add).then_inc(s_resb, 1)
                    hold(s_slot, (b + 1) * TOP)
                    for k in range(TOP):
                        for t in range(NT):
                            pool.indirect_dma_start(
                                routed[:, :], bass.IndirectOffsetOnAxis(ap=slot_index[k][:, t:t + 1], axis=0),
                                rows[k][:, t, :], None).then_inc(s_scat, 16)
                pool.wait_ge(s_tail, 1)
                for e in range(E):
                    pool.indirect_dma_start(
                        routed[:, :], bass.IndirectOffsetOnAxis(ap=tail_index[:, e:e + 1], axis=0),
                        zero_row[:], None).then_inc(s_tailout, 16)
                pool.wait_ge(s_scat, 16 * TOP * NT * B)
                pool.wait_ge(s_tailout, 16 * (E + 1))

            @block.scalar
            def _(act):
                act.sem_inc(s_turned, 2)
                act.sem_inc(s_rounded, 3)
                act.sem_inc(s_e, 2)
                TURNS = 3 * NT

                def copy_turned(b, n):
                    act.wait_ge(s_turn, b * TURNS + n + 1)
                    act.activation(xT[:, n % 2], turn_bank[n % 2][:, 0:D].rearrange("p (c m) -> p c m", c=DC),
                                   ACT.Copy).then_inc(s_turned, 1)

                def copy_round(b, n, k, dst):
                    act.wait_ge(s_round, b * BR + n + 1)
                    act.activation(dst, round_bank[k % 3][:, :], ACT.Copy).then_inc(s_rounded, 1)

                def prep(b, n, k, par):
                    for i, dst in enumerate((KT[par], KT[par], QT, QT)):
                        h = i % 2
                        copy_round(b, n + i, k + i, dst[:, h * 512:(h + 1) * 512])

                def with_max(b, n, k):
                    for h in range(2):
                        copy_round(b, n + h, k + h, QTm[:, h * 512:(h + 1) * 512])

                def exps(g):
                    for u in range(UNITS):
                        kt = u // 2
                        act.wait_ge(s_s2, g * UNITS + u + 1)
                        act.wait_ge(s_pv, g * NT + kt + 1)
                        act.activation(probs[:, u % 4, kt * P:S], S2[u % 2][:, kt * P:S], ACT.Exp,
                                       scale=float(HD) ** -0.5).then_inc(s_e, 1)

                with act.Fori(0, B, 1) as b:
                    for t in range(NT):
                        copy_turned(b, t)
                    prep(b, 0, 0, 0)
                    with_max(b, 4, 4)
                    prep(b, 6, 6, 1)
                    with act.Fori(0, PAIRS // 2 - 1, 1) as i:
                        for par in range(2):
                            s = 2 * i + par
                            exps(b * PAIRS + s)
                            with_max(b, 10 + 6 * s, 10)
                            prep(b, 12 + 6 * s, 12, par)
                    exps(b * PAIRS + PAIRS - 2)
                    with_max(b, BR - 2, BR - 2)
                    exps(b * PAIRS + PAIRS - 1)
                    for n in range(NT, TURNS):
                        copy_turned(b, n)
                    act.wait_ge(s_soft, b + 1)
                    act.activation(R["exps"][:], R["work"][:], ACT.Exp).then_inc(s_softed, 1)

            @block.vector
            def _(dve):
                chain = Chain(dve, s_chain, 0)
                link = chain.link
                for i in range(2):
                    for t_ in (Qa[i], Ka[i]):
                        link(dve.memset(t_[:].bitcast(F32), 0.0))
                for i in range(2):
                    dve.memset(Ka[i][:, :, :, PRODUCTS:SCORED].bitcast(F32), 1.0)
                dve.memset(maxima[:], LOWEST).then_inc(s_dconst, 1)
                link(dve.memset(running[:], 0.0))
                link(dve.memset(same_expert[:], 1.0))
                link(dve.memset(same_expert[:, :, 0:1], 0.0))
                dve.wait_ge(s_const, 13)
                link(dve.tensor_scalar(e_start[:], e_index[:], float(REGION), None, ALU.mult))
                link(dve.tensor_scalar(zero_row[:, D:D + 1].bitcast(I32), token[:, 0:1], 0.0, float(NOWHERE),
                                       ALU.mult, ALU.add))
                dve.wait_ge(s_wq, 16 * 7)
                for c in range(DC):
                    link(dve.tensor_scalar(router[:, c], router_raw[:, c], scale_raw[:, c:c + 1], None, ALU.mult))
                for e in range(E):
                    link(dve.tensor_scalar(R["scale"][:, e], e_index[:, e], 0.0, escale[:, e:e + 1],
                                           ALU.mult, ALU.add))
                dve.sem_inc(s_dconst, 1)
                dve.sem_inc(s_qkv, 2)
                dve.sem_inc(s_s1r, 2)
                dve.sem_inc(s_o, 1)
                fixed = chain.n

                def rsqrt():
                    link(dve.tensor_single_scalar(newton[:].bitcast(I32), var[:].bitcast(I32), 1,
                                                  op=ALU.arith_shift_right))
                    link(dve.tensor_scalar(rstd[:].bitcast(I32), newton[:].bitcast(I32), -1.0,
                                           float(RSQRT_MAGIC), ALU.mult, ALU.add))
                    for _ in range(3):
                        link(dve.tensor_tensor(newton[:], rstd[:], rstd[:], ALU.mult))
                        link(dve.scalar_tensor_tensor(out=newton[:], in0=newton[:], scalar=-0.5, in1=var[:],
                                                      op0=ALU.mult, op1=ALU.mult))
                        link(dve.scalar_tensor_tensor(out=rstd[:], in0=newton[:], scalar=1.5, in1=rstd[:],
                                                      op0=ALU.add, op1=ALU.mult))

                def row_stats(src):
                    for t in range(NT):
                        dve.bn_stats(stats[:, t], src[:, t]).then_inc(s_chain, 1)
                    chain.n += NT
                    dve.wait_ge(s_chain, chain.base + chain.n)
                    dve.sem_inc(s_dve_passed, 1)
                    for t in range(NT):
                        dve.bn_aggr(moments[:, t], stats[:, t]).then_inc(s_chain, 1)
                    chain.n += NT
                    dve.wait_ge(s_chain, chain.base + chain.n)
                    link(dve.tensor_scalar(var[:], moments[:, :, 1], 1e-5, None, ALU.add))
                    rsqrt()

                def reduce_maxima(g, par, s):
                    c = 0
                    for j in range(2):
                        for qt in range(NT):
                            for piece in range(1 if qt < HALF else 2):
                                n = min((qt + 1) * P - piece * 512, 512)
                                dve.wait_ge(s_s1, g * CHUNKS + c + 1)
                                dve.tensor_reduce(maxima[:, j, qt, piece:piece + 1], S1[c % 2][:, 0:n], AX.X,
                                                  ALU.max).then_inc(s_s1r, 1)
                                c += 1
                    dve.wait_ge(s_s1r, 2 + (g + 1) * CHUNKS)
                    dve.tensor_reduce(top_score[:], maxima[:], AX.X, ALU.max).then_inc(s_mstep, 1)
                    dve.wait_ge(s_mstep, g * 2 + 1)
                    top = top_score[:].rearrange("p j t -> p t j")
                    hi = Qa[par][:, :, :, PRODUCTS]
                    dve.tensor_scalar(hi, top, -1.0, None, ALU.mult).then_inc(s_mstep, 1)
                    dve.wait_ge(s_mstep, g * 2 + 2)
                    dve.scalar_tensor_tensor(out=Qa[par][:, :, :, PRODUCTS + 1], in0=top, scalar=-1.0,
                                             in1=hi.bitcast(F32), op0=ALU.mult,
                                             op1=ALU.subtract).then_inc(s_m, 1)

                def normalise(g, s):
                    dve.wait_ge(s_pv, 2 + (g + 1) * NT)
                    dve.tensor_copy(OT[:], OB[:]).then_inc(s_o, 1)
                    dve.wait_ge(s_ot, g + 1)
                    turned = TB[:, :].rearrange("p (u g r) -> p u g r", u=HALF, g=4)
                    dve.reciprocal(rden[:], turned[:, :, :, HD]).then_inc(s_nstep, 1)
                    dve.wait_ge(s_nstep, g + 1)
                    for h in range(2):
                        dst = attn[:, h * HALF:(h + 1) * HALF, ds(s * 2 * HD, 2 * HD)]
                        last = dve.tensor_tensor(
                            dst.rearrange("p u (j d) -> p u j d", j=2),
                            turned[:, :, 2 * h:2 * h + 2, 0:HD],
                            rden[:, :, 2 * h:2 * h + 2].unsqueeze(3).to_broadcast([P, HALF, 2, HD]), ALU.mult)
                    last.then_inc(s_norm, 1)

                def add_bias(b, t):
                    dve.wait_ge(s_qkvp, b * NT + t + 1)
                    dve.tensor_tensor(qkv[:, t], S2[t % 2][:, 0:3 * D], qkv_bias[:], ALU.add).then_inc(s_qkv, 1)

                def over_e(v):
                    return v[:].unsqueeze(1).to_broadcast([P, E, NT])

                def by_token(r):
                    return r[:].rearrange("p e t -> p t e")

                def route(b):
                    work = R["work"]
                    junk = probs[:, 0:TOP, :].rearrange("p a (t d) -> p (a t) d", d=D)
                    for t in range(NT):
                        h = rows[0][:, t, 0:D]
                        dve.tensor_tensor_reduce(junk[:, t], h, h, 1.0, 0.0, ALU.mult, ALU.add,
                                                 V1["sum"][:, t:t + 1]).then_inc(s_chain, 1)
                    chain.n += NT
                    dve.wait_ge(s_chain, chain.base + chain.n)
                    link(dve.tensor_scalar(var[:], V1["sum"][:], 1.0 / D, 1e-6, ALU.mult, ALU.add))
                    rsqrt()
                    link(dve.tensor_scalar(V1["w"][:], rstd[:], float(D) ** -0.5, None, ALU.mult))
                    dve.wait_ge(s_logit, b + 1)
                    link(dve.tensor_tensor(R["logits"][:], S2[0][:, 0:NT * E].rearrange("p (t e) -> p e t", e=E),
                                           over_e(V1["w"]), ALU.mult))
                    for k in range(TOP):
                        left, pick = R["logits" if k == 0 else "left"], R[f"pick{k}"]
                        link(dve.tensor_reduce(V1["best"][:], by_token(left), AX.X, ALU.max))
                        if k == 0:
                            link(dve.tensor_tensor(work[:], left[:], over_e(V1["best"]), ALU.subtract))
                            dve.sem_inc(s_soft, 1)
                            dve.wait_ge(s_softed, b + 1)
                        link(dve.tensor_tensor(work[:], left[:], over_e(V1["best"]), ALU.is_equal))
                        link(dve.scalar_tensor_tensor(out=work[:], in0=work[:], scalar=-float(E), in1=e_index[:],
                                                      op0=ALU.mult, op1=ALU.add))
                        link(dve.tensor_reduce(V1["index"][:], by_token(work), AX.X, ALU.min))
                        link(dve.tensor_tensor(pick[:], work[:], over_e(V1["index"]), ALU.is_equal))
                        if k == 0:
                            link(dve.scalar_tensor_tensor(out=R["left"][:], in0=pick[:], scalar=LOWEST,
                                                          in1=left[:], op0=ALU.mult, op1=ALU.add))
                    link(dve.tensor_tensor(R["chosen"][:], R["pick0"][:], R["pick1"][:], ALU.add))
                    link(dve.tensor_tensor_scan(R["count"][:].rearrange("p e t -> p (e t)"),
                                                same_expert[:].rearrange("p e t -> p (e t)"),
                                                R["chosen"][:].rearrange("p e t -> p (e t)"), 0.0,
                                                ALU.mult, ALU.add))
                    dve.sem_inc(s_chosen, 1)
                    exps = R["exps"]
                    link(dve.tensor_reduce(V1["sum"][:], by_token(exps), AX.X, ALU.add))
                    link(dve.reciprocal(V1["rsum"][:], V1["sum"][:]))
                    link(dve.tensor_tensor(exps[:], exps[:], over_e(V1["rsum"]), ALU.mult))
                    link(dve.tensor_tensor(work[:], exps[:], R["chosen"][:], ALU.mult))
                    link(dve.tensor_reduce(V1["gate"][:], by_token(work), AX.X, ALU.add))
                    link(dve.tensor_scalar(V1["flag"][:], V1["gate"][:], 0.0, None, ALU.is_le))
                    link(dve.tensor_tensor(V1["gate"][:], V1["gate"][:], V1["flag"][:], ALU.add))
                    link(dve.reciprocal(V1["rsum"][:], V1["gate"][:]))
                    link(dve.tensor_tensor(exps[:], exps[:], over_e(V1["rsum"]), ALU.mult))
                    link(dve.tensor_tensor(exps[:], exps[:], R["scale"][:], ALU.mult))
                    dve.wait_ge(s_rank, b + 1)
                    link(dve.tensor_tensor(tail_f[:], running[:], e_start[:, :, 0], ALU.add))
                    link(dve.tensor_tensor(R["slot"][:], S2[1][:, 0:E * NT].rearrange("p (e t) -> p e t", t=NT),
                                           tail_f[:].unsqueeze(2).to_broadcast([P, E, NT]), ALU.add))
                    link(dve.tensor_tensor(running[:], S2[1][:, 512:512 + E], running[:], ALU.add))
                    for k in range(TOP):
                        link(dve.tensor_tensor(work[:], R[f"pick{k}"][:], exps[:], ALU.mult))
                        link(dve.tensor_reduce(rows[k][:, :, D + 1], by_token(work), AX.X, ALU.add))
                        link(dve.tensor_scalar(rows[k][:, :, D].bitcast(I32), token[:], float(k * T), None, ALU.add))
                        link(dve.tensor_tensor(work[:], R[f"pick{k}"][:], R["slot"][:], ALU.mult))
                        link(dve.tensor_reduce(V1["dest"][:], by_token(work), AX.X, ALU.add))
                        dve.tensor_copy(slot_index[k][:], V1["dest"][:]).then_inc(s_slot, 1)
                        dve.wait_ge(s_slot, b * TOP + k + 1)
                    link(dve.tensor_scalar(token[:], token[:], float(S), None, ALU.add))

                per_batch = 2 * (2 * NT + 1 + 11) + NT + (NT + 1 + 11 + 1 + 1) + (2 * 5 + 2) + 2 + 10 + 3 + 2 * 5 + 1
                chain.per_round, chain.fixed = per_batch, fixed

                with dve.Fori(0, B, 1) as b:
                    chain.begin(b)
                    dve.wait_ge(s_x, (b + 1) * 16)
                    row_stats(xin)
                    for t in range(NT):
                        if t >= 2:
                            dve.wait_ge(s_turn, b * 3 * NT + t - 1)
                        last = dve.tensor_scalar(xn[:, t % 2], xin[:, t], moments[:, t, 0:1], rstd[:, t:t + 1],
                                                 ALU.subtract, ALU.mult)
                        last.then_inc(s_xn, 1)
                        if t >= 1:
                            add_bias(b, t - 1)
                    add_bias(b, NT - 1)
                    reduce_maxima(b * PAIRS, 0, 0)
                    with dve.Fori(0, PAIRS // 2 - 1, 1) as i:
                        for par in range(2):
                            s = 2 * i + par
                            reduce_maxima(b * PAIRS + s + 1, 1 - par, s + 1)
                            normalise(b * PAIRS + s, s)
                    reduce_maxima(b * PAIRS + PAIRS - 1, 1, PAIRS - 1)
                    normalise(b * PAIRS + PAIRS - 2, PAIRS - 2)
                    normalise(b * PAIRS + PAIRS - 1, PAIRS - 1)
                    dve.wait_ge(s_resb, b + 1)
                    for t in range(NT):
                        dve.wait_ge(s_proj, b * NT + t + 1)
                        dve.tensor_tensor(xres[:, t], S1[t % 2][:, 0:D], xres[:, t], ALU.add).then_inc(s_x2, 1)
                    dve.wait_ge(s_x2, (b + 1) * NT)
                    row_stats(xres)
                    dve.wait_ge(s_scat, b * 16 * TOP * NT)
                    for t in range(NT):
                        for k in range(TOP):
                            last = dve.tensor_scalar(rows[k][:, t, 0:D], xres[:, t], moments[:, t, 0:1],
                                                     rstd[:, t:t + 1], ALU.subtract, ALU.mult)
                        last.then_inc(s_chain, 1)
                    chain.n += NT
                    dve.wait_ge(s_chain, chain.base + chain.n)
                    dve.sem_inc(s_h, 1)
                    route(b)
                    chain.end()

                chain.begin(B)
                link(dve.tensor_tensor(tail_f[:], running[:], e_start[:, :, 0], ALU.add))
                link(dve.tensor_scalar(tail_index[:], tail_f[:], token[:, 0:1], -float(T), ALU.add, ALU.add))
                dve.sem_inc(s_tail, 1)


            @block.tensor
            def _(pe):
                pe.sem_inc(s_pv, 2)
                pe.wait_ge(s_const, 13)
                pe.wait_ge(s_dconst, 2)
                TURNS = 3 * NT

                def turn(b, n, src):
                    pe.wait_ge(s_turned, b * TURNS + n + 1)
                    for c in range(DC):
                        last = pe.transpose(turn_bank[n % 2][:, c * P:(c + 1) * P], src[:, c * P:(c + 1) * P],
                                            ident[:])
                    last.then_inc(s_turn, 1)

                def project(b, t):
                    pe.wait_ge(s_turned, 2 + b * TURNS + t + 1)
                    pe.wait_ge(s_qkv, b * NT + t + 1)
                    for lo in (0, 512):
                        n = min(3 * D - lo, 512)
                        for c in range(DC):
                            last = pe.matmul(S2[t % 2][:, lo:lo + n], xT[:, t % 2, c], wqkv[:, c, lo:lo + n],
                                             start=(c == 0), stop=(c == DC - 1))
                    last.then_inc(s_qkvp, 1)

                def round_(b, n, k, src, half):
                    pe.wait_ge(s_rounded, b * BR + n + 1)
                    bank = round_bank[k % 3]
                    for i in range(HALF):
                        tile = src[:, half * HALF + i].rearrange("p j r -> p (j r)").bitcast(F32)
                        last = pe.transpose(bank[:, i * P:(i + 1) * P], tile, ident[:])
                    last.then_inc(s_round, 1)

                def prep(b, n, k, par, pairs_scored):
                    pe.wait_ge(s_build, pairs_scored + 1)
                    pe.wait_ge(s_s1r, 2 + pairs_scored * CHUNKS)
                    for i in range(4):
                        round_(b, n + i, k + i, (Ka[par], Qa[par])[i // 2], i % 2)

                def with_max(b, n, k, par, pairs_scored):
                    pe.wait_ge(s_m, pairs_scored)
                    for i in range(2):
                        round_(b, n + i, k + i, Qa[par], i)

                def scores(g, par, c, rounds):
                    pieces = [(j, qt, piece) for j in range(2) for qt in range(NT)
                              for piece in range(1 if qt < HALF else 2)]
                    j, qt, piece = pieces[c]
                    lo = piece * 512
                    n = min((qt + 1) * P - lo, 512)
                    diagonal = lo + n == (qt + 1) * P
                    if c == 0:
                        pe.wait_ge(s_rounded, 3 + rounds)
                    pe.wait_ge(s_s1r, g * CHUNKS + c + 1)
                    r = slice(j * ROWS, j * ROWS + PRODUCTS)
                    last = pe.matmul(S1[c % 2][:, 0:n], QT[r, qt * P:(qt + 1) * P], KT[par][r, lo:lo + n],
                                     start=True, stop=not diagonal)
                    if diagonal:
                        last = pe.matmul(S1[c % 2][:, n - P:n], identb[:], mask_qk[:], start=False, stop=True)
                    last.then_inc(s_s1, 1)

                def shifted(g, par, u):
                    kt, j = u // 2, u % 2
                    pe.wait_ge(s_e, g * UNITS + u + 1)
                    r = slice(j * ROWS, j * ROWS + SCORED)
                    for lo, hi in ((kt * P, 512), (max(512, kt * P), S)):
                        if lo >= hi:
                            continue
                        diagonal = lo == kt * P
                        last = pe.matmul(S2[u % 2][:, lo:hi], KT[par][r, kt * P:(kt + 1) * P], QTm[r, lo:hi],
                                         start=True, stop=not diagonal)
                        if diagonal:
                            last = pe.matmul(S2[u % 2][:, lo:lo + P], identb[:], mask_kq[:], start=False, stop=True)
                    last.then_inc(s_s2, 1)

                def values(g, b, s, par, kt):
                    pe.wait_ge(s_e, 2 + g * UNITS + 2 * kt + 2)
                    if kt == 0:
                        pe.wait_ge(s_o, g + 1)
                        pe.wait_ge(s_v, g + 1)
                    for h in range(2):
                        lo, hi = max(h * 512, kt * P), (h + 1) * 512
                        if lo >= hi:
                            continue
                        for j in range(2):
                            q = 32 * (2 * h + j)
                            last = pe.matmul(OB[q:q + 32, lo - h * 512:512], V[par][:, kt, j],
                                             probs[:, (2 * kt + j) % 4, lo:hi], start=(kt == 0),
                                             stop=(kt == HALF * (h + 1) - 1))
                    last.then_inc(s_pv, 1)

                def turn_output(g, rounds):
                    pe.wait_ge(s_o, 1 + g + 1)
                    pe.wait_ge(s_rounded, 3 + rounds)
                    for i in range(HALF):
                        last = pe.transpose(TB[:, i * P:(i + 1) * P], OT[:, i * P:(i + 1) * P], ident[:])
                    last.then_inc(s_ot, 1)

                def project_out(b, t):
                    n = NT + t
                    pe.wait_ge(s_turned, 2 + b * TURNS + n + 1)
                    if t >= 2:
                        pe.wait_ge(s_x2, b * NT + t - 1)
                    for c in range(DC):
                        last = pe.matmul(S1[t % 2][:, 0:D], xT[:, n % 2, c], wout[:, c],
                                         start=(c == 0), stop=(c == DC - 1))
                    last.then_inc(s_proj, 1)

                def router_logits(b, t):
                    n = 2 * NT + t
                    pe.wait_ge(s_turned, 2 + b * TURNS + n + 1)
                    for c in range(DC):
                        last = pe.matmul(S2[0][:, t * E:(t + 1) * E], xT[:, n % 2, c], router[:, c],
                                         start=(c == 0), stop=(c == DC - 1))
                    if t == NT - 1:
                        last.then_inc(s_logit, 1)

                def slot(b, s, par, next_scores, next_prep):
                    g = b * PAIRS + s
                    rounds = b * BR + (10 + 6 * s if next_scores else BR)
                    pe.wait_ge(s_rounded, 3 + rounds)
                    c = 0
                    for u in range(UNITS):
                        shifted(g, par, u)
                        while next_scores and c < min(2 * (u + 1), CHUNKS):
                            scores(g + 1, 1 - par, c, rounds)
                            c += 1
                        if u % 2 and u >= 3:
                            values(g, b, s, par, u // 2 - 1)
                    pe.wait_ge(s_norm, g)
                    if next_scores:
                        with_max(b, 10 + 6 * s, 10, 1 - par, g + 2)
                    values(g, b, s, par, NT - 1)
                    if next_prep:
                        prep(b, 12 + 6 * s, 12, par, g + 2)
                    turn_output(g, b * BR + (16 + 6 * s if next_prep else BR))

                pe.wait_ge(s_wq, 16 * 7)
                with pe.Fori(0, B, 1) as b:
                    pe.wait_ge(s_slot, b * TOP)
                    for t in range(NT):
                        pe.wait_ge(s_xn, b * NT + t + 1)
                        turn(b, t, xn[:, t % 2])
                        if t >= 1:
                            project(b, t - 1)
                    project(b, NT - 1)
                    prep(b, 0, 0, 0, b * PAIRS)
                    for c in range(CHUNKS):
                        scores(b * PAIRS, 0, c, b * BR + 4)
                    with_max(b, 4, 4, 0, b * PAIRS + 1)
                    prep(b, 6, 6, 1, b * PAIRS + 1)
                    with pe.Fori(0, PAIRS // 2 - 1, 1) as i:
                        for par in range(2):
                            slot(b, 2 * i + par, par, True, True)
                    slot(b, PAIRS - 2, 0, True, False)
                    slot(b, PAIRS - 1, 1, False, False)
                    pe.wait_ge(s_norm, (b + 1) * PAIRS)
                    for t in range(NT):
                        turn(b, NT + t, attn[:, t])
                        if t >= 1:
                            project_out(b, t - 1)
                    project_out(b, NT - 1)
                    pe.wait_ge(s_h, b + 1)
                    for t in range(NT):
                        turn(b, 2 * NT + t, rows[0][:, t, 0:D])
                        if t >= 1:
                            router_logits(b, t - 1)
                    router_logits(b, NT - 1)
                    pe.wait_ge(s_chosen, b + 1)
                    flat = R["count"][:].rearrange("p e t -> p (e t)")
                    pe.matmul(S2[1][:, 0:E * NT], not_before[:], R["chosen"][:].rearrange("p e t -> p (e t)"),
                              start=True, stop=False)
                    pe.matmul(S2[1][:, 0:E * NT], ones[:], flat, start=False, stop=True)
                    pe.matmul(S2[1][:, 512:512 + E], ones[:], R["count"][:, :, NT - 1],
                              start=True, stop=True).then_inc(s_rank, 1)

        xe = rows[0]
        ye = rows[1]
        gelu_ = probs[:, 0:2, 0:HID]
        acts = probs[:, 0:2, HID:2 * HID]
        actT = probs[:, 2:4, 0:HID]
        RING = 4
        assert MT % RING == 0
        q_wl = sem("linear_in"); q_iota = sem("step_constants"); q_table = sem("table_made"); q_tstep = sem("table_step")
        q_xe = [sem(f"expert_rows_in{r}") for r in range(RING)]
        q_out = [sem(f"expert_rows_out{r}") for r in range(RING)]
        q_xt = sem("expert_x_turned"); q_xtc = sem("expert_x_copied"); q_g = sem("gates_summed")
        q_gelu = sem("gelu_ready"); q_act = sem("act_ready"); q_at = sem("act_turned"); q_atc = sem("act_copied")
        q_dn = sem("down_summed"); q_y = sem("y_ready")

        with nc.Block() as block:

            @block.sync
            def _(sp):
                for c in range(HC):
                    sp.dma_start(wl[:, c], linear_w[:, c * P:(c + 1) * P, :].rearrange("e p d -> p e d"))\
                        .then_inc(q_wl, 16)
                sp.wait_ge(q_table, 1)
                with sp.Fori(0, MT // RING, 1) as q:
                    for r in range(RING):
                        row = sp.value_load(table_row[0:1, ds(q * RING + r, 1)], min_val=0, max_val=ZEROS)
                        sp.wait_ge(q_out[r], q * 16)
                        sp.dma_start(xe[:, r, :], routed[ds(row, P), :]).then_inc(q_xe[r], 16)
                sp.wait_ge(q_wl, 16 * HC)

            @block.gpsimd
            def _(pool):
                pool.iota(step_index[:], pattern=[[1, MT]], base=0, channel_multiplier=0,
                          allow_small_or_imprecise_dtypes=True).then_inc(q_iota, 1)
                pool.iota(tile_start[:], pattern=[[P, T // P]], base=0, channel_multiplier=0,
                          allow_small_or_imprecise_dtypes=True).then_inc(q_iota, 1)
                with pool.Fori(0, MT // RING, 1) as q:
                    for r in range(RING):
                        pool.wait_ge(q_y, 2 + q * RING + r + 1)
                        pool.sem_inc(s_pool_passed, 1)
                        pool.indirect_dma_start(
                            expert_out[:, :], bass.IndirectOffsetOnAxis(ap=xe[:, r, D:D + 1].bitcast(I32), axis=0),
                            ye[:, r, 0:D], None, bounds_check=TOP * T - 1, oob_is_err=False).then_inc(q_out[r], 16)
                for r in range(RING):
                    pool.wait_ge(q_out[r], 16 * (MT // RING))

            @block.scalar
            def _(act):
                act.sem_inc(q_xtc, 1)
                act.sem_inc(q_atc, 1)

                def copy_x(i, r):
                    act.wait_ge(q_xt, i + 1)
                    act.activation(xT[:, r % 2], TB[:, 0:D].rearrange("p (c m) -> p c m", c=DC),
                                   ACT.Copy).then_inc(q_xtc, 1)

                def gelu(i, r):
                    act.wait_ge(q_g, i + 1)
                    act.wait_ge(q_act, i + 1)
                    act.activation(gelu_[:, r % 2], S2[r % 2][:, 0:HID], ACT.Gelu_apprx_tanh).then_inc(q_gelu, 1)

                def copy_act(i, r):
                    act.wait_ge(q_at, 2 + i + 1)
                    act.activation(actT[:, r % 2], OB[:, 0:HID], ACT.Copy).then_inc(q_atc, 1)

                def group(base, last):
                    for r in range(RING):
                        i = base + r
                        if not (last and r >= RING - 2):
                            copy_x(i + 2, r)
                        copy_act(i, r)
                        if not (last and r == RING - 1):
                            gelu(i + 1, r + 1)

                copy_x(0, 0)
                gelu(0, 0)
                copy_x(1, 1)
                with act.Fori(0, MT // RING - 1, 1) as q:
                    group(q * RING, False)
                group(MT - RING, True)

            @block.vector
            def _(dve):
                dve.sem_inc(q_act, 2)
                dve.sem_inc(q_y, 2)
                chain = Chain(dve, q_tstep, 0)
                link = chain.link
                most = T // P
                step = xres[0:1].rearrange("p t d -> p (t d)")
                big = probs[0:1].rearrange("p a n -> p (a n)")
                sizes = big[:, 0:E * most].rearrange("p (e j) -> p e j", e=E)
                reached = big[:, 1024:1024 + MT * E].rearrange("p (s e) -> p s e", e=E)
                weighed = step[:, 0:MT * E].rearrange("p (s e) -> p s e", e=E)
                small = xin[0:1].rearrange("p t d -> p (t d)")
                tiles, ends = small[:, 0:E], small[:, E:2 * E]
                count, which, first, local = (small[:, 64 + n * MT:64 + (n + 1) * MT] for n in range(4))
                dve.wait_ge(q_iota, 2)
                link(dve.tensor_tensor(sizes, running[0:1].unsqueeze(2).to_broadcast([1, E, most]),
                                       tile_start[:].unsqueeze(1).to_broadcast([1, E, most]), ALU.is_gt))
                link(dve.tensor_reduce(tiles, sizes, AX.X, ALU.add))
                link(dve.tensor_tensor_scan(ends, ones[0:1, 0:E], tiles, 0.0, ALU.mult, ALU.add))
                link(dve.tensor_tensor(reached, step_index[:].unsqueeze(2).to_broadcast([1, MT, E]),
                                       ends.unsqueeze(1).to_broadcast([1, MT, E]), ALU.is_ge))
                link(dve.tensor_reduce(which, reached, AX.X, ALU.add))
                link(dve.tensor_tensor(weighed, reached, tiles.unsqueeze(1).to_broadcast([1, MT, E]), ALU.mult))
                link(dve.tensor_reduce(first, weighed, AX.X, ALU.add))
                link(dve.tensor_tensor(local, step_index[:], first, ALU.subtract))
                link(dve.tensor_scalar(count, which, float(E), float(P), ALU.is_lt, ALU.mult))
                link(dve.tensor_tensor(local, local, count, ALU.mult))
                link(dve.scalar_tensor_tensor(out=table_row[:], in0=which, scalar=float(REGION), in1=local,
                                              op0=ALU.mult, op1=ALU.add))
                link(dve.tensor_scalar(table_expert[:], which, float(E - 1), None, ALU.min))
                dve.sem_inc(q_table, 1)

                def multiply(i, r):
                    dve.wait_ge(q_gelu, i + 1)
                    dve.wait_ge(q_at, i + 1)
                    dve.tensor_tensor(acts[:, r % 2], gelu_[:, r % 2], S2[r % 2][:, HID:2 * HID],
                                      ALU.mult).then_inc(q_act, 1)

                def weigh(i, q, r):
                    dve.wait_ge(q_dn, i + 1)
                    dve.wait_ge(q_out[r], q * 16)
                    dve.tensor_scalar(ye[:, r, 0:D], S1[r % 2][:, 0:D], xe[:, r, D + 1:D + 2], None,
                                      ALU.mult).then_inc(q_y, 1)

                def group(q, base, last):
                    for r in range(RING):
                        if not (last and r == RING - 1):
                            multiply(base + r + 1, r + 1)
                        weigh(base + r, q, r)

                multiply(0, 0)
                with dve.Fori(0, MT // RING - 1, 1) as q:
                    group(q, q * RING, False)
                group(MT // RING - 1, MT - RING, True)

            @block.tensor
            def _(pe):
                pe.sem_inc(q_at, 2)
                pe.wait_ge(q_table, 1)

                def expert(i):
                    return pe.value_load(table_expert[0:1, ds(i, 1)], min_val=0, max_val=E - 1)

                def turn_x(i, q, r):
                    pe.wait_ge(q_xe[r], 16 * (q + 1))
                    pe.wait_ge(q_xtc, i + 1)
                    for c in range(DC):
                        last = pe.transpose(TB[:, c * P:(c + 1) * P], xe[:, r, c * P:(c + 1) * P], ident[:])
                    last.then_inc(q_xt, 1)

                def gates(i, r):
                    e = expert(i)
                    pe.wait_ge(q_xtc, 1 + i + 1)
                    pe.wait_ge(q_act, i + 1)
                    for n in range(2):
                        for c in range(DC):
                            w = wg[:, c, ds(e, 1), n * HID:(n + 1) * HID].rearrange("p a h -> p (a h)")
                            last = pe.matmul(S2[r % 2][:, n * HID:(n + 1) * HID], xT[:, r % 2, c], w,
                                             start=(c == 0), stop=(c == DC - 1))
                    last.then_inc(q_g, 1)

                def turn_act(i, r):
                    pe.wait_ge(q_act, 2 + i + 1)
                    pe.wait_ge(q_atc, i + 1)
                    for c in range(HC):
                        last = pe.transpose(OB[:, c * P:(c + 1) * P], acts[:, r % 2, c * P:(c + 1) * P], ident[:])
                    last.then_inc(q_at, 1)

                def down(i, r):
                    e = expert(i)
                    pe.wait_ge(q_atc, 1 + i + 1)
                    pe.wait_ge(q_y, i + 1)
                    for c in range(HC):
                        w = wl[:, c, ds(e, 1), :].rearrange("p a d -> p (a d)")
                        last = pe.matmul(S1[r % 2][:, 0:D], actT[:, r % 2, c * P:(c + 1) * P], w,
                                         start=(c == 0), stop=(c == HC - 1))
                    last.then_inc(q_dn, 1)

                def group(q, base, last):
                    for r in range(RING):
                        i = base + r
                        if not (last and r == RING - 1):
                            gates(i + 1, r + 1)
                        if not (last and r >= RING - 2):
                            turn_x(i + 2, q + (r + 2) // RING, (r + 2) % RING)
                        turn_act(i, r)
                        down(i, r)

                turn_x(0, 0, 0)
                gates(0, 0)
                turn_x(1, 0, 1)
                pe.wait_ge(q_wl, 16 * HC)
                with pe.Fori(0, MT // RING - 1, 1) as q:
                    group(q, q * RING, False)
                group(MT // RING - 1, MT - RING, True)

        f_in = [sem(f"final_in{i}") for i in range(2)]
        f_out = [sem(f"final_out{i}") for i in range(2)]
        f_step = sem("final_step")
        f_done = [sem(f"final_done{i}") for i in range(2)]
        parts = [[v.rearrange("p t d -> p (t d)") for v in (xres[:], xin[:])],
                 [shared[:, n * NT * D:(n + 1) * NT * D] for n in (0, 1)],
                 [shared[:, n * NT * D:(n + 1) * NT * D] for n in (2, 3)]]
        assert B % 2 == 0

        def tiled(v):
            return v.rearrange("p (t d) -> p t d", t=NT)

        with nc.Block() as block:

            @block.sync
            def _(sp):
                with sp.Fori(0, B // 2, 1) as i:
                    for m in range(2):
                        b = 2 * i + m
                        sp.wait_ge(f_out[m], i * 16)
                        for n, src in enumerate((x2_rows[b], expert_rows[0, b], expert_rows[1, b])):
                            sp.dma_start(tiled(parts[n][m]), src).then_inc(f_in[m], 16)

            @block.vector
            def _(dve):
                with dve.Fori(0, B // 2, 1) as i:
                    for m in range(2):
                        dve.wait_ge(f_in[m], (i + 1) * 48)
                        dve.tensor_tensor(parts[0][m], parts[0][m], parts[1][m], ALU.add).then_inc(f_step, 1)
                        dve.wait_ge(f_step, 2 * i + m + 1)
                        dve.tensor_tensor(parts[0][m], parts[0][m], parts[2][m], ALU.add).then_inc(f_done[m], 1)

            @block.scalar
            def _(act):
                with act.Fori(0, B // 2, 1) as i:
                    for m in range(2):
                        act.wait_ge(f_done[m], i + 1)
                        act.dma_start(out_rows[2 * i + m], tiled(parts[0][m])).then_inc(f_out[m], 16)
                for m in range(2):
                    act.wait_ge(f_out[m], 16 * (B // 2))


def kernel(L0_attn_x, L0_attn_qkv_w, L0_attn_qkv_b, L0_attn_out_w, L0_attn_out_b, L0_ffn_router_scale,
           L0_ffn_router_w, L0_ffn_gating_w, L0_ffn_linear_w, L0_ffn_per_expert_scale):
    import numpy as np
    import concourse.bacc as bacc
    from concourse.bass_utils import run_bass_kernel_spmd

    nc = bacc.Bacc("TRN2", target_bir_lowering=False, num_devices=1)
    given = {"x": L0_attn_x, "qkv_w": L0_attn_qkv_w, "qkv_b": L0_attn_qkv_b, "out_w": L0_attn_out_w,
             "out_b": L0_attn_out_b, "router_scale": L0_ffn_router_scale, "router_w": L0_ffn_router_w,
             "gate_w": np.transpose(np.asarray(L0_ffn_gating_w), (3, 0, 1, 2)), "linear_w": L0_ffn_linear_w,
             "expert_scale": L0_ffn_per_expert_scale}
    arrays, args = {}, []
    for name, value in given.items():
        a = np.ascontiguousarray(value)
        arrays[name] = a
        args.append(nc.dram_tensor(name, a.shape, mybir.dt.from_np(a.dtype), kind="ExternalInput").ap())
    shape = arrays["x"].shape
    args.append(nc.dram_tensor("out", shape, F32, kind="ExternalOutput").ap())
    preln_attention_then_routed_ffn(nc, *args)
    return run_bass_kernel_spmd(nc, [arrays], core_ids=[0]).results[0]["out"]
```

```python
import concourse.bass as bass
from concourse import mybir
from contextlib import ExitStack

F32 = mybir.dt.float32
F32R = mybir.dt.float32r
BF16 = mybir.dt.bfloat16
I32 = mybir.dt.int32
ALU = mybir.AluOpType
ACT = mybir.ActivationFunctionType
AX = mybir.AxisListType
ds = bass.ds

P = 128
HEADS = 16
HD = 16
D = HEADS * HD
ROWS = 64
PRODUCTS = 3 * HD
SCORED = PRODUCTS + 2
E = 8
TOP = 2
MASKED = -1e30
LOWEST = -3e38
RSQRT_MAGIC = 0x5F3759DF
ROW = D + 2


class Chain:

    def __init__(self, engine, sem, per_round, fixed=0):
        self.engine, self.sem, self.per_round, self.n, self.fixed = engine, sem, per_round, 0, fixed
        self.base = fixed

    def begin(self, round_):
        self.base, self.n = round_ * self.per_round + self.fixed, 0

    def link(self, instruction):
        self.n += 1
        instruction.then_inc(self.sem, 1)
        self.engine.wait_ge(self.sem, self.base + self.n)

    def end(self):
        assert self.n == self.per_round, (self.n, self.per_round)


def preln_attention_then_routed_ffn(
    nc: bass.Bass,
    x: bass.AP,
    qkv_w: bass.AP,
    qkv_b: bass.AP,
    out_w: bass.AP,
    out_b: bass.AP,
    router_scale: bass.AP,
    router_w: bass.AP,
    gate_w: bass.AP,
    linear_w: bass.AP,
    expert_scale: bass.AP,
    out: bass.AP,
):
    B, S, _ = x.shape
    HID = linear_w.shape[1]
    T = B * S
    NT = S // P
    HALF = NT // 2
    HC = HID // P
    DC = D // P
    PAIRS = HEADS // 2
    REGION = T + P
    ZEROS = E * REGION
    MT = TOP * T // P + E
    AHEAD = 2
    NOWHERE = 1 << 20
    UNITS = 2 * NT
    CHUNKS = 2 * (HALF + 2 * (NT - HALF))
    ROUNDS = 6
    BR = PAIRS * ROUNDS

    x_rows = x.rearrange("b (t p) d -> b p t d", p=P)
    out_rows = out.rearrange("b (t p) d -> b p t d", p=P)
    x2_dram = nc.dram_tensor("x2_dram", [B, S, D], F32, kind="Internal").ap()
    x2_rows = x2_dram.rearrange("b (t p) d -> b p t d", p=P)
    routed = nc.dram_tensor("routed", [ZEROS + P, ROW], F32, kind="Internal").ap()
    expert_out = nc.dram_tensor("expert_out", [TOP * T, D], F32, kind="Internal").ap()
    expert_rows = expert_out.rearrange("(k b t p) d -> k b p t d", k=TOP, b=B, p=P)

    with ExitStack() as ctx:
        def sb(name, shape, dt=F32):
            return ctx.enter_context(nc.sbuf_tensor(name, shape, dt))

        def sem(name):
            return ctx.enter_context(nc.semaphore(name))

        TILES = NT * D
        shared = sb("shared", [P, 12 * TILES])
        qkv_all = shared[:, 0:2 * NT * 3 * D].rearrange("p (t n) -> p t n", n=3 * D)
        attn = shared[:, NT * 6 * D:NT * 7 * D].rearrange("p (t n) -> p t n", t=NT)
        turned_all = shared[:, NT * 7 * D:NT * 8 * D].rearrange("p (c s) -> p c s", c=DC)
        probs = shared[:, 8 * TILES:10 * TILES].rearrange("p (n s) -> p n s", s=S)
        xres = shared[:, 10 * TILES:11 * TILES].rearrange("p (t d) -> p t d", t=NT)
        wqkv = shared[:, 11 * TILES:11 * TILES + DC * 3 * D].rearrange("p (c n) -> p c n", c=DC)
        wout = shared[:, 12 * TILES - DC * D:12 * TILES].rearrange("p (c n) -> p c n", c=DC)
        wg = [shared[:, c * E * 2 * HID:(c + 1) * E * 2 * HID].rearrange("p (e n) -> p e n", e=E) for c in range(DC)]
        wl = shared[:, DC * E * 2 * HID:].rearrange("p (c e d) -> p c e d", c=HC, e=E)
        assert DC == 2 and HC == 4 and 4 * S == 2 * TILES and E * 2 * HID == 4 * TILES and E * D == TILES
        assert DC * 4 * D == TILES and B % 2 == 0
        qkv_bias = sb("qkv_bias", [P, 3 * D])
        out_bias = sb("out_bias", [P, D])
        xin = sb("xin", [P, HALF, D])
        xn = sb("xn", [P, 2, D])
        xT = sb("xT", [P, 2, DC, P])
        Qa = [sb(f"Qa{i}", [P, NT, 2, ROWS], F32R) for i in range(2)]
        Ka = sb("Ka", [P, NT, 2, ROWS], F32R)
        V = [sb(f"V{i}", [P, NT, 2, 32]) for i in range(2)]
        KT = [sb(f"KT{i}", [P, S], F32R) for i in range(2)]
        QT = [[sb(f"QT{i}_{j}", [P, S], F32R) for j in range(2)] for i in range(2)]
        QTm = [[sb(f"QTm{i}_{j}", [P, S], F32R) for j in range(2)] for i in range(2)]
        OT = sb("OT", [P, 4 * P])
        work = sb("work", [P, 3, 2 * HID])
        rows = [sb(f"rows{k}", [P, NT, ROW]) for k in range(TOP)]
        ident = sb("ident", [P, P])
        identb = sb("identb", [P, P], BF16)
        mask_qk = sb("mask_qk", [P, P], BF16)
        mask_kq = sb("mask_kq", [P, P], BF16)
        not_before = sb("not_before", [P, P])
        ones = sb("ones", [P, P])
        maxima = sb("maxima", [P, 2, NT, 2])
        top_score = sb("top_score", [P, 2, NT])
        rden = sb("rden", [P, HALF, 4])
        scale_raw = sb("scale_raw", [P, DC])
        router_raw = sb("router_raw", [P, DC, E])
        router = sb("router", [P, DC, E])
        escale = sb("escale", [P, E])
        e_index = sb("e_index", [P, E, NT])
        e_start = sb("e_start", [P, E])
        same_expert = sb("same_expert", [P, E, NT])
        token = sb("token", [P, NT])
        running = sb("running", [P, E])
        norm1 = {n: sb("n1_" + n, [P, HALF] + w) for n, w in
                 (("stats", [6]), ("moments", [2]), ("var", []), ("rstd", []), ("newton", []))}
        norm2 = {n: sb("n2_" + n, [P, NT] + w) for n, w in
                 (("stats", [6]), ("moments", [2]), ("var", []), ("rstd", []), ("newton", []))}
        R = {n: sb("r_" + n, [P, E, NT]) for n in
             ("logits", "left", "pick0", "pick1", "chosen", "count", "slot", "exps", "work")}
        V1 = {n: sb("v_" + n, [P, NT]) for n in ("best", "index", "sum", "rsum", "gate", "flag", "w", "dest")}
        slot_index = [sb(f"slot_index{k}", [P, NT], I32) for k in range(TOP)]
        tail_f = sb("tail_f", [P, E])
        tail_index = sb("tail_index", [P, E], I32)
        table_row = sb("table_row", [1, MT], I32)
        table_expert = sb("table_expert", [1, MT], I32)
        step_index = sb("step_index", [1, MT])
        tile_start = sb("tile_start", [1, T // P])

        def pb(name, n):
            return ctx.enter_context(nc.psum_tensor(name, [P, n], F32))
        S2 = [pb(f"S2_{i}", 512) for i in range(3)]
        S1 = [pb(f"S1_{i}", 512) for i in range(3)]
        TB = pb("TB", 512)
        OB = pb("OB", 512)

        s_wq = sem("weights_in"); s_wg = sem("gate_weights_in")
        s_const = sem("constants_made"); s_dconst = sem("vector_constants")
        s_x = sem("x_in"); s_res = sem("residual_in"); s_resb = sem("residual_biased")
        s_xn = sem("xn_ready"); s_xturn = sem("x_turned"); s_xcopy = sem("x_turned_copied")
        s_aturn = sem("attn_turned"); s_acopy = sem("attn_turned_copied")
        s_hturn = sem("h_turned"); s_hcopy = sem("h_turned_copied")
        s_qkvp = sem("qkv_summed"); s_qkv = sem("qkv_ready")
        s_build = sem("qk_rows_built"); s_v = sem("v_built"); s_pool = sem("pool_step"); s_set = sem("pool_setup")
        s_round = sem("round_turned"); s_q = sem("q_copied"); s_k = sem("k_copied")
        s_s1 = sem("scores_ready"); s_s1r = sem("scores_reduced"); s_m = sem("maxima_in_rows"); s_mstep = sem("max_step")
        s_s2 = sem("shifted_scores_ready"); s_e = sem("probs_ready"); s_pv = sem("pv_done")
        s_o = sem("o_copied"); s_ot = sem("o_turned"); s_norm = sem("o_normalised"); s_nstep = sem("norm_step")
        s_proj = sem("projected"); s_x2 = sem("x2_ready"); s_h = sem("h_ready"); s_logit = sem("logits_summed")
        s_soft = sem("router_shifted"); s_softed = sem("router_exps")
        s_chosen = sem("chosen_ready"); s_rank = sem("ranks_summed");
        s_slot = sem("slots_ready")
        s_scat = sem("rows_scattered"); s_listed = sem("rows_in_lists"); s_x2out = sem("x2_stored"); s_link1 = sem("norm1_step")
        s_link2 = sem("norm2_step"); s_setup = sem("vector_setup"); s_end = sem("vector_end")
        s_pool_passed = sem("pool_waits_passed"); s_dve_passed = sem("vector_waits_passed")
        s_tail = sem("tail_ready"); s_tailout = sem("tails_zeroed")

        PIECES = [(j, qt, piece) for j in range(2) for qt in range(NT) for piece in range(1 if qt < HALF else 2)]
        SCORE_UNITS = range(1, UNITS - 4)

        STARTUP = 3 * NT + CHUNKS
        PARTS = [(u, max(h * 512, u // 2 * P), (h + 1) * 512) for u in range(UNITS)
                 for h in range(0 if u // 2 < HALF else 1, 2)]
        NP = len(PARTS)
        assert NP % 3 == 0 and CHUNKS % 3 == 0

        def parts_before(u):
            return sum(1 for v, _, _ in PARTS if v < u)

        def beside_before(s, u):
            return 3 * sum(projected_at(s, v) is not None or (s, v) in (ROUTER_AT, RANK_AT) for v in range(u))

        def beside_bank(u, i):
            return S1[(pieces_after(u) + i) % 3]

        def s1_position(b, s):
            return STARTUP + b * (PAIRS * CHUNKS + 3 * (NT + 2)) + s * CHUNKS + 3 * (2 * min(max(s - 1, 0), NT // 2)
                                                                               + (s > 6))

        def piece_keys(c):
            j, qt, piece = PIECES[c]
            return min((qt + 1) * P - piece * 512, 512)

        def pieces_after(u):
            unit_columns = [S - v // 2 * P for v in SCORE_UNITS]
            share = sum(n for v, n in zip(SCORE_UNITS, unit_columns) if v <= u) / sum(unit_columns)
            total, c, reached = sum(piece_keys(c) for c in range(CHUNKS)), 0, 0
            while c < CHUNKS and reached < share * total:
                reached += piece_keys(c)
                c += 1
            return c

        def projected_at(s, u):
            return 2 * (s - 1) + (u == 11) if 1 <= s <= NT // 2 and u in (5, 11) else None

        def turned_at(s, u):
            return 2 * (s - 1) + (u == 8) if 1 <= s <= NT // 2 and u in (3, 8) else None

        def attn_turned_at(s, u):
            return u - 4 if s == 0 and 4 <= u < 4 + NT else None

        def h_turned_at(s, u):
            return u - 3 if s == 6 and 3 <= u < 3 + NT else None

        ROUTER_AT, RANK_AT = (6, 11), (7, 9)
        MAX_AT, Q_AT, MAX_TURN_AT = 12, (12, 14), (14, 15)
        assert len(PIECES) == CHUNKS and PAIRS == 8 and NT == 8
        G = B * PAIRS
        RSQRT_LINKS = 11
        ROUTE_LINKS = (NT + (NT + 1 + RSQRT_LINKS) + NT * (TOP + 1) + (NT + 2 + RSQRT_LINKS + 1)
                       + 1 + 2 + 5 + 5 + 2 + 10 + 3 + TOP * 5 + 1)
        WEIGHT_LOADS = 4 + HC
        zero_row = rows[0][:, 0, :]

        def sequences(engine, sequence):
            sequence(0, False, True)
            with engine.Fori(1, B - 1, 1) as b:
                sequence(b, True, True)
            sequence(B - 1, True, False)

        with nc.Block() as block:

            @block.sync
            def _(sp):
                sp.dma_start(xin[:], x_rows[0, :, 0:HALF]).then_inc(s_x, 16)
                sp.dma_start(wqkv[:], qkv_w.rearrange("(c p) n -> p c n", p=P)).then_inc(s_wq, 16)
                sp.dma_start(qkv_bias[:], qkv_b.partition_broadcast(P)).then_inc(s_wq, 16)
                sp.dma_start(wout[:], out_w.rearrange("(c p) n -> p c n", p=P)).then_inc(s_wq, 16)
                sp.dma_start(out_bias[:], out_b.partition_broadcast(P)).then_inc(s_wq, 16)
                sp.dma_start(scale_raw[:], router_scale.rearrange("(c p) -> p c", p=P),
                             allow_slow_non_contiguous=True).then_inc(s_wq, 16)
                sp.dma_start(router_raw[:], router_w.rearrange("(c p) e -> p c e", p=P)).then_inc(s_wq, 16)
                sp.dma_start(escale[:], expert_scale.partition_broadcast(P)).then_inc(s_wq, 16)

                def load_x(b, half):
                    sp.wait_ge(s_xn, b * NT + half * HALF)
                    sp.dma_start(xin[:], x_rows[b, :, half * HALF:(half + 1) * HALF]).then_inc(s_x, 16)

                def residual(b):
                    sp.dma_start(xres[:], x_rows[b]).then_inc(s_res, 16)

                def store(b):
                    sp.wait_ge(s_x2, (b + 1) * NT)
                    sp.dma_start(x2_rows[b], xres[:]).then_inc(s_x2out, 16)
                    sp.wait_ge(s_x2out, (b + 1) * 16)
                    sp.wait_ge(s_h, b + 1)

                def sequence(b, before, behind):
                    if behind:
                        load_x(b + 1, 0)
                        load_x(b + 1, 1)
                    if before:
                        store(b - 1)
                    residual(b)

                load_x(0, 1)
                def load_gates(c, first, last):
                    sp.dma_start(wg[c][:, first:last],
                                 gate_w[c * P:(c + 1) * P, first:last].rearrange("p e g h -> p e (g h)"))\
                        .then_inc(s_wg, 16)

                def load_linear(c):
                    sp.dma_start(wl[:, c], linear_w[:, c * P:(c + 1) * P, :].rearrange("e p d -> p e d"))\
                        .then_inc(s_wg, 16)

                sequence(0, False, True)
                with sp.Fori(1, B - 1, 1) as b:
                    sequence(b, True, True)
                sp.wait_ge(s_build, (B - 1) * PAIRS)
                sp.wait_ge(s_v, (B - 1) * PAIRS)
                load_gates(0, 0, 6)
                sequence(B - 1, True, False)
                sp.wait_ge(s_build, G)
                sp.wait_ge(s_v, G)
                load_gates(0, 6, 8)
                load_gates(1, 0, 4)
                sp.wait_ge(s_pv, 2 + G * NT)
                load_linear(0)
                load_linear(1)
                sp.wait_ge(s_proj, B * NT)
                load_linear(3)
                store(B - 1)
                load_linear(2)
                sp.wait_ge(s_logit, B)
                load_gates(1, 4, 8)

            @block.gpsimd
            def _(pool):
                chain = Chain(pool, s_set, 0)
                link = chain.link
                link(pool.memset(ident[:], 0.0))
                pool.affine_select(out=ident[:], in_=ident[:], compare_op=ALU.not_equal, fill=1.0, base=0,
                                   pattern=[[-1, P]], channel_multiplier=1).then_inc(s_const, 1)
                link(pool.memset(identb[:], 0.0))
                pool.affine_select(out=identb[:], in_=identb[:], compare_op=ALU.not_equal, fill=1.0, base=0,
                                   pattern=[[-1, P]], channel_multiplier=1).then_inc(s_const, 1)
                link(pool.memset(mask_qk[:], 0.0))
                pool.affine_select(out=mask_qk[:], in_=mask_qk[:], compare_op=ALU.is_ge, fill=MASKED, base=0,
                                   pattern=[[-1, P]], channel_multiplier=1).then_inc(s_const, 1)
                link(pool.memset(mask_kq[:], 0.0))
                pool.affine_select(out=mask_kq[:], in_=mask_kq[:], compare_op=ALU.is_ge, fill=MASKED, base=0,
                                   pattern=[[1, P]], channel_multiplier=-1).then_inc(s_const, 1)
                link(pool.memset(not_before[:], 0.0))
                pool.affine_select(out=not_before[:], in_=not_before[:], compare_op=ALU.is_gt, fill=-1.0, base=0,
                                   pattern=[[1, P]], channel_multiplier=-1).then_inc(s_const, 1)
                pool.memset(ones[:], 1.0).then_inc(s_const, 1)
                pool.iota(e_index[:], pattern=[[1, E], [0, NT]], base=0, channel_multiplier=0,
                          allow_small_or_imprecise_dtypes=True).then_inc(s_const, 1)
                pool.iota(token[:], pattern=[[P, NT]], base=0, channel_multiplier=1,
                          allow_small_or_imprecise_dtypes=True).then_inc(s_const, 1)
                for i in range(2):
                    pool.memset(V[i][:], 0.0).then_inc(s_const, 1)
                pool.wait_ge(s_const, 10)
                for i in range(2):
                    pool.memset(V[i][:, :, :, HD:HD + 1], 1.0).then_inc(s_const, 1)
                pool.wait_ge(s_dconst, 1)

                def hold(semaphore, value):
                    pool.wait_ge(semaphore, value)
                    pool.sem_inc(s_pool_passed, 1)

                def of_pair(b, which, s):
                    tiles = qkv_all[:, ds(b % 2 * NT, NT), which * D + s * 2 * HD:which * D + (s + 1) * 2 * HD]
                    return tiles.rearrange("p t (j d) -> p t j d", j=2)

                def build_qk(g, b, s, par):
                    for n, (dst, which, hi, lo) in enumerate(((Qa[par], 0, (0, 1), 2), (Ka, 1, (0, 2), 1))):
                        src = of_pair(b, which, s)
                        for m in hi:
                            pool.tensor_copy(dst[:, :, :, m * HD:(m + 1) * HD], src).then_inc(s_pool, 1)
                        if n == 0:
                            pool.memset(dst[:, :, :, PRODUCTS:SCORED].bitcast(F32), 0.0).then_inc(s_pool, 1)
                        hold(s_pool, g * 5 + (3 if n == 0 else 5))
                        last = pool.tensor_tensor(dst[:, :, :, lo * HD:(lo + 1) * HD], src,
                                                  dst[:, :, :, 0:HD].bitcast(F32), ALU.subtract)
                    last.then_inc(s_build, 1)

                def build_v(b, s, par):
                    pool.tensor_copy(V[par][:, :, :, 0:HD], of_pair(b, 2, s)).then_inc(s_v, 1)

                def scatter(t):
                    for k in range(TOP):
                        pool.indirect_dma_start(
                            routed[:, :], bass.IndirectOffsetOnAxis(ap=slot_index[k][:, t:t + 1], axis=0),
                            rows[k][:, t, :], None).then_inc(s_scat, 16)

                def bias_residual(b):
                    hold(s_res, (b + 1) * 16)
                    pool.tensor_tensor(xres[:], xres[:], out_bias[:].unsqueeze(1).to_broadcast([P, NT, D]),
                                       ALU.add).then_inc(s_resb, 1)

                def slot(b, s, before, behind):
                    g, par = b * PAIRS + s, s % 2
                    if s < PAIRS - 2 or behind:
                        b2, s2 = (b, s + 2) if s < PAIRS - 2 else (b + 1, s + 2 - PAIRS)
                        if s == PAIRS - 2:
                            hold(s_qkv, b + 2)
                        hold(s_round, g * ROUNDS + 10)
                        build_qk(g + 2, b2, s2, par)
                    if s < PAIRS - 1 or behind:
                        b1, s1 = (b, s + 1) if s < PAIRS - 1 else (b + 1, 0)
                        hold(s_pv, 2 + g * NT)
                        build_v(b1, s1, 1 - par)
                    if before and s == 0:
                        bias_residual(b - 1)

                def sequence(b, before, behind, routed_before):
                    for s in range(PAIRS):
                        slot(b, s, before, behind)
                        if s < NT // 2 and routed_before:
                            if s == 0:
                                hold(s_slot, (b - 1) * TOP)
                            scatter(2 * s)
                            scatter(2 * s + 1)
                        if s == NT // 2:
                            if routed_before:
                                hold(s_scat, (b - 1) * 16 * TOP * NT)
                            pool.sem_inc(s_listed, 1)

                hold(s_qkv, 1)
                build_qk(0, 0, 0, 0)
                build_v(0, 0, 0)
                hold(s_round, 2)
                build_qk(1, 0, 1, 1)
                sequence(0, False, True, False)
                sequence(1, True, True, False)
                with pool.Fori(2, B - 1, 1) as b:
                    sequence(b, True, True, True)
                sequence(B - 1, True, False, True)
                bias_residual(B - 1)
                for b in (B - 2, B - 1):
                    hold(s_slot, (b + 1) * TOP)
                    for t in range(NT):
                        scatter(t)
                    pool.wait_ge(s_scat, (b + 1) * 16 * TOP * NT)
                    pool.sem_inc(s_listed, 1)
                hold(s_tail, 1)
                pool.dma_start(routed[ZEROS:ZEROS + P, :], zero_row).then_inc(s_tailout, 16)
                for e in range(E):
                    pool.indirect_dma_start(
                        routed[:, :], bass.IndirectOffsetOnAxis(ap=tail_index[:, e:e + 1], axis=0),
                        zero_row, None).then_inc(s_tailout, 16)
                pool.wait_ge(s_tailout, 16 * (E + 1))

            @block.scalar
            def _(act):
                act.sem_inc(s_xcopy, 1)
                act.sem_inc(s_acopy, 1)
                act.sem_inc(s_hcopy, 1)
                act.sem_inc(s_e, 3)
                act.sem_inc(s_o, 1)
                turned = TB[:, 0:D].rearrange("p (c m) -> p c m", c=DC)

                def copy_x(b, t):
                    act.wait_ge(s_xturn, b * NT + t + 1)
                    act.activation(xT[:, t % 2], turned, ACT.Copy).then_inc(s_xcopy, 1)

                def copy_to_all(b, t, ready, copied):
                    act.wait_ge(ready, b * NT + t + 1)
                    act.activation(turned_all[:, :, t * P:(t + 1) * P], turned, ACT.Copy).then_inc(copied, 1)

                def copy_q(n, bank, dst, half):
                    act.wait_ge(s_round, n + 1)
                    for j in range(2):
                        r = slice(j * ROWS, (j + 1) * ROWS)
                        last = act.activation(dst[j][r, half * 512:(half + 1) * 512], bank[r, :], ACT.Copy)
                    last.then_inc(s_q, 1)

                def exps(g, u):
                    kt = u // 2
                    act.wait_ge(s_pv, g * NT + kt + 1)
                    for n, (v, lo, hi) in enumerate(PARTS):
                        if v == u:
                            act.wait_ge(s_s2, g * NP + n + 1)
                            act.activation(probs[:, u % 4, lo:hi], S2[n % 3][:, lo % 512:(hi - 1) % 512 + 1],
                                           ACT.Exp, scale=float(HD) ** -0.5).then_inc(s_e, 1)

                def copy_o(g):
                    act.wait_ge(s_pv, 2 + (g + 1) * NT)
                    act.activation(OT[:], OB[:], ACT.Copy).then_inc(s_o, 1)

                def sequence(b, before, behind):
                    for s in range(PAIRS):
                        g = b * PAIRS + s
                        for u in range(UNITS):
                            exps(g, u)
                            if before and attn_turned_at(s, u) is not None:
                                copy_to_all(b - 1, attn_turned_at(s, u), s_aturn, s_acopy)
                            if before and h_turned_at(s, u) is not None:
                                copy_to_all(b - 1, h_turned_at(s, u), s_hturn, s_hcopy)
                            if behind and turned_at(s, u) is not None:
                                copy_x(b + 1, turned_at(s, u))
                            if before and (s, u) == (7, 3):
                                router_exps(b - 1)
                            if u == 0 and (s or before):
                                copy_o(g - 1)
                            if u in Q_AT and (s < PAIRS - 2 or behind):
                                half = Q_AT.index(u)
                                copy_q(10 + g * ROUNDS + half, TB, QT[s % 2], half)
                            if u in MAX_TURN_AT and (s < PAIRS - 1 or behind):
                                half = MAX_TURN_AT.index(u)
                                copy_q(12 + g * ROUNDS + half if s < PAIRS - 2 or behind
                                       else 10 + g * ROUNDS + half, S1[half], QTm[1 - s % 2], half)

                def router_exps(b):
                    act.wait_ge(s_soft, b + 1)
                    act.activation(R["exps"][:], R["work"][:], ACT.Exp).then_inc(s_softed, 1)

                for t in range(NT):
                    copy_x(0, t)
                copy_q(2, S1[1], QT[0], 0)
                copy_q(3, TB, QT[0], 1)
                copy_q(4, S1[0], QTm[0], 0)
                copy_q(5, S1[1], QTm[0], 1)
                copy_q(6, TB, QT[1], 0)
                copy_q(7, TB, QT[1], 1)
                sequences(act, sequence)
                copy_o(G - 1)
                for t in range(NT):
                    copy_to_all(B - 1, t, s_aturn, s_acopy)
                for t in range(NT):
                    copy_to_all(B - 1, t, s_hturn, s_hcopy)
                router_exps(B - 1)

            @block.vector
            def _(dve):
                setup = Chain(dve, s_setup, 0)
                link = setup.link
                for t_ in (Qa[0], Qa[1], Ka, *QT[0], *QT[1], *QTm[0], *QTm[1]):
                    link(dve.memset(t_[:].bitcast(F32), 0.0))
                link(dve.memset(Ka[:, :, :, PRODUCTS:SCORED].bitcast(F32), 1.0))
                link(dve.memset(maxima[:], LOWEST))
                dve.sem_inc(s_dconst, 1)
                link(dve.memset(running[:], 0.0))
                link(dve.memset(same_expert[:], 1.0))
                link(dve.memset(same_expert[:, :, 0:1], 0.0))
                dve.wait_ge(s_const, 12)
                link(dve.tensor_scalar(e_start[:], e_index[:, :, 0], float(REGION), None, ALU.mult))
                dve.sem_inc(s_s1r, 3)
                dve.sem_inc(s_norm, 1)

                def rsqrt(link, n):
                    var, rstd, newton = n["var"], n["rstd"], n["newton"]
                    link(dve.tensor_single_scalar(newton[:].bitcast(I32), var[:].bitcast(I32), 1,
                                                  op=ALU.arith_shift_right))
                    link(dve.tensor_scalar(rstd[:].bitcast(I32), newton[:].bitcast(I32), -1.0,
                                           float(RSQRT_MAGIC), ALU.mult, ALU.add))
                    for _ in range(3):
                        link(dve.tensor_tensor(newton[:], rstd[:], rstd[:], ALU.mult))
                        link(dve.scalar_tensor_tensor(out=newton[:], in0=newton[:], scalar=-0.5, in1=var[:],
                                                      op0=ALU.mult, op1=ALU.mult))
                        link(dve.scalar_tensor_tensor(out=rstd[:], in0=newton[:], scalar=1.5, in1=rstd[:],
                                                      op0=ALU.add, op1=ALU.mult))

                def together(chain, instructions):
                    for last in instructions:
                        last.then_inc(chain.sem, 1)
                        chain.n += 1
                    dve.wait_ge(chain.sem, chain.base + chain.n)
                    dve.sem_inc(s_dve_passed, 1)

                def moments(chain, n, tiles):
                    together(chain, (dve.bn_aggr(n["moments"][:, t], n["stats"][:, t]) for t in range(tiles)))

                norm1_chain = Chain(dve, s_link1, 2 * (HALF + HALF + 1 + 11))

                def first_norm(b, half):
                    chain = norm1_chain
                    if half == 0:
                        chain.begin(b)
                    dve.wait_ge(s_x, (2 * b + half + 1) * 16)
                    together(chain, (dve.bn_stats(norm1["stats"][:, t], xin[:, t]) for t in range(HALF)))
                    moments(chain, norm1, HALF)
                    chain.link(dve.tensor_scalar(norm1["var"][:], norm1["moments"][:, :, 1], 1e-5, None, ALU.add))
                    rsqrt(chain.link, norm1)
                    if half == 1:
                        chain.end()

                def normalise_x(b, t):
                    i = t % HALF
                    if t >= 2:
                        dve.wait_ge(s_xturn, b * NT + t - 1)
                    dve.tensor_scalar(xn[:, t % 2], xin[:, i], norm1["moments"][:, i, 0:1],
                                      norm1["rstd"][:, i:i + 1], ALU.subtract, ALU.mult).then_inc(s_xn, 1)

                def add_bias(b, t, uses, banks):
                    dst = qkv_all[:, ds(b % 2 * NT + t, 1), :].rearrange("p a n -> p (a n)")
                    for i, (lo, hi) in enumerate(((0, 512), (512, 3 * D))):
                        dve.wait_ge(s_qkvp, (b * NT + t) * 2 + i + 1)
                        dve.tensor_tensor(dst[:, lo:hi], banks[i][:, 0:hi - lo], qkv_bias[:, lo:hi],
                                          ALU.add).then_inc(s_s1r, 1 if i == 0 else uses - 1)

                def reduce_piece(g, c):
                    j, qt, piece = PIECES[c]
                    n = min((qt + 1) * P - piece * 512, 512)
                    dve.wait_ge(s_s1, g * CHUNKS + c + 1)
                    dve.tensor_reduce(maxima[:, j, qt, piece:piece + 1], S1[c % 3][:, 0:n], AX.X,
                                      ALU.max).then_inc(s_s1r, 1)

                def maxima_to_rows(g, par, position):
                    dve.wait_ge(s_s1r, 3 + position)
                    dve.tensor_reduce(top_score[:], maxima[:], AX.X, ALU.max).then_inc(s_mstep, 1)
                    dve.wait_ge(s_mstep, g * 2 + 1)
                    top = top_score[:].rearrange("p j t -> p t j")
                    hi = Qa[par][:, :, :, PRODUCTS]
                    dve.tensor_scalar(hi, top, -1.0, None, ALU.mult).then_inc(s_mstep, 1)
                    dve.wait_ge(s_mstep, g * 2 + 2)
                    dve.scalar_tensor_tensor(out=Qa[par][:, :, :, PRODUCTS + 1], in0=top, scalar=-1.0,
                                             in1=hi.bitcast(F32), op0=ALU.mult,
                                             op1=ALU.subtract).then_inc(s_m, 1)

                def copy_k(n, bank, par, half):
                    dve.wait_ge(s_round, n + 1)
                    dve.tensor_copy(KT[par][:, half * 512:(half + 1) * 512], bank[:]).then_inc(s_k, 1)

                def normalise(g, s):
                    dve.wait_ge(s_ot, g + 1)
                    turned = TB[:, :].rearrange("p (u g r) -> p u g r", u=HALF, g=4)
                    dve.reciprocal(rden[:], turned[:, :, :, HD]).then_inc(s_nstep, 1)
                    dve.wait_ge(s_nstep, g + 1)
                    for h in range(2):
                        dst = attn[:, h * HALF:(h + 1) * HALF, s * 2 * HD:(s + 1) * 2 * HD]
                        last = dve.tensor_tensor(
                            dst.rearrange("p u (j d) -> p u j d", j=2),
                            turned[:, :, 2 * h:2 * h + 2, 0:HD],
                            rden[:, :, 2 * h:2 * h + 2].unsqueeze(3).to_broadcast([P, HALF, 2, HD]), ALU.mult)
                    last.then_inc(s_norm, 1)

                norm2_chain = Chain(dve, s_link2, ROUTE_LINKS)
                link2 = norm2_chain.link

                def over_e(v):
                    return v[:].unsqueeze(1).to_broadcast([P, E, NT])

                def by_token(r):
                    return r[:].rearrange("p e t -> p t e")

                def residual(b, t, bank):
                    if t == 0:
                        norm2_chain.begin(b)
                        dve.wait_ge(s_resb, b + 1)
                    dve.wait_ge(s_proj, b * NT + t + 1)
                    dve.tensor_tensor(xres[:, t], bank[:, 0:D], xres[:, t], ALU.add).then_inc(s_x2, 1)
                    dve.wait_ge(s_x2, b * NT + t + 1)
                    dve.bn_stats(norm2["stats"][:, t], xres[:, t]).then_inc(s_link2, 1)
                    norm2_chain.n += 1

                def second_norm():
                    dve.wait_ge(s_link2, norm2_chain.base + norm2_chain.n)
                    dve.sem_inc(s_dve_passed, 1)
                    moments(norm2_chain, norm2, NT)
                    link2(dve.tensor_scalar(norm2["var"][:], norm2["moments"][:, :, 1], 1e-5, None, ALU.add))
                    rsqrt(link2, norm2)

                def normalise_rows(t):
                    together(norm2_chain, (
                        dve.tensor_scalar(rows[k][:, t, 0:D], xres[:, t], norm2["moments"][:, t, 0:1],
                                          norm2["rstd"][:, t:t + 1], ALU.subtract, ALU.mult) for k in range(TOP)))
                    dve.bn_stats(norm2["stats"][:, t], rows[0][:, t, 0:D]).then_inc(s_link2, 1)
                    norm2_chain.n += 1

                def rms():
                    dve.wait_ge(s_link2, norm2_chain.base + norm2_chain.n)
                    dve.sem_inc(s_h, 1)
                    dve.sem_inc(s_dve_passed, 1)
                    moments(norm2_chain, norm2, NT)
                    mean, var = norm2["moments"][:, :, 0], norm2["moments"][:, :, 1]
                    link2(dve.tensor_tensor(norm2["newton"][:], mean, mean, ALU.mult))
                    link2(dve.scalar_tensor_tensor(out=norm2["var"][:], in0=norm2["newton"][:], scalar=1e-6, in1=var,
                                                   op0=ALU.add, op1=ALU.add))
                    rsqrt(link2, norm2)
                    link2(dve.tensor_scalar(V1["w"][:], norm2["rstd"][:], float(D) ** -0.5, None, ALU.mult))

                def logits(b, bank):
                    dve.wait_ge(s_logit, b + 1)
                    link2(dve.tensor_tensor(R["logits"][:], bank[:, 0:NT * E].rearrange("p (t e) -> p e t", e=E),
                                            over_e(V1["w"]), ALU.mult))
                    dve.sem_inc(s_s1r, 3)

                def pick(k):
                    left, work, chosen = R["logits" if k == 0 else "left"], R["work"], R[f"pick{k}"]
                    if k == 1:
                        link2(dve.tensor_reduce(V1["best"][:], by_token(left), AX.X, ALU.max))
                    link2(dve.tensor_tensor(work[:], left[:], over_e(V1["best"]), ALU.is_equal))
                    link2(dve.scalar_tensor_tensor(out=work[:], in0=work[:], scalar=-float(E), in1=e_index[:],
                                                   op0=ALU.mult, op1=ALU.add))
                    link2(dve.tensor_reduce(V1["index"][:], by_token(work), AX.X, ALU.min))
                    link2(dve.tensor_tensor(chosen[:], work[:], over_e(V1["index"]), ALU.is_equal))
                    if k == 0:
                        link2(dve.scalar_tensor_tensor(out=R["left"][:], in0=chosen[:], scalar=LOWEST,
                                                       in1=left[:], op0=ALU.mult, op1=ALU.add))

                def shift_logits():
                    link2(dve.tensor_reduce(V1["best"][:], by_token(R["logits"]), AX.X, ALU.max))
                    link2(dve.tensor_tensor(R["work"][:], R["logits"][:], over_e(V1["best"]), ALU.subtract))
                    dve.sem_inc(s_soft, 1)

                def choose(b):
                    dve.wait_ge(s_softed, b + 1)
                    pick(0)
                    pick(1)
                    link2(dve.tensor_tensor(R["chosen"][:], R["pick0"][:], R["pick1"][:], ALU.add))
                    link2(dve.tensor_tensor_scan(R["count"][:].rearrange("p e t -> p (e t)"),
                                                 same_expert[:].rearrange("p e t -> p (e t)"),
                                                 R["chosen"][:].rearrange("p e t -> p (e t)"), 0.0,
                                                 ALU.mult, ALU.add))
                    dve.sem_inc(s_chosen, 1)

                def weights():
                    exps, work = R["exps"], R["work"]
                    link2(dve.tensor_reduce(V1["sum"][:], by_token(exps), AX.X, ALU.add))
                    link2(dve.reciprocal(V1["rsum"][:], V1["sum"][:]))
                    link2(dve.tensor_tensor(exps[:], exps[:], over_e(V1["rsum"]), ALU.mult))
                    link2(dve.tensor_tensor(work[:], exps[:], R["chosen"][:], ALU.mult))
                    link2(dve.tensor_reduce(V1["gate"][:], by_token(work), AX.X, ALU.add))
                    link2(dve.tensor_scalar(V1["flag"][:], V1["gate"][:], 0.0, None, ALU.is_le))
                    link2(dve.tensor_tensor(V1["gate"][:], V1["gate"][:], V1["flag"][:], ALU.add))
                    link2(dve.reciprocal(V1["rsum"][:], V1["gate"][:]))
                    link2(dve.tensor_tensor(exps[:], exps[:], over_e(V1["rsum"]), ALU.mult))
                    link2(dve.tensor_tensor(exps[:], exps[:], escale[:].unsqueeze(2).to_broadcast([P, E, NT]),
                                            ALU.mult))

                def ranks(b, bank):
                    dve.wait_ge(s_rank, b + 1)
                    link2(dve.tensor_tensor(tail_f[:], running[:], e_start[:], ALU.add))
                    link2(dve.tensor_tensor(R["slot"][:], bank[:, 0:E * NT].rearrange("p (e t) -> p e t", t=NT),
                                            tail_f[:].unsqueeze(2).to_broadcast([P, E, NT]), ALU.add))
                    link2(dve.tensor_tensor(running[:], bank[:, E * NT:E * NT + E], running[:], ALU.add))
                    dve.sem_inc(s_s1r, 3)

                def places(b):
                    work = R["work"]
                    for k in range(TOP):
                        link2(dve.tensor_tensor(work[:], R[f"pick{k}"][:], exps_[:], ALU.mult))
                        link2(dve.tensor_reduce(rows[k][:, :, D + 1], by_token(work), AX.X, ALU.add))
                        link2(dve.tensor_scalar(rows[k][:, :, D].bitcast(I32), token[:], float(k * T), None, ALU.add))
                        link2(dve.tensor_tensor(work[:], R[f"pick{k}"][:], R["slot"][:], ALU.mult))
                        link2(dve.tensor_reduce(V1["dest"][:], by_token(work), AX.X, ALU.add))
                        dve.tensor_copy(slot_index[k][:], V1["dest"][:]).then_inc(s_slot, 1)
                        dve.wait_ge(s_slot, b * TOP + k + 1)
                    link2(dve.tensor_scalar(token[:], token[:], float(S), None, ALU.add))
                    norm2_chain.end()

                exps_ = R["exps"]

                def beside(b, s, u, before, behind):
                    if behind:
                        if (s, u) == (0, 10):
                            first_norm(b + 1, 0)
                        if 1 <= s <= 4 and u < 2:
                            normalise_x(b + 1, 2 * (s - 1) + u)
                        if (s, u) == (2, 13):
                            first_norm(b + 1, 1)
                    t = projected_at(s, u)
                    if t is not None:
                        if behind:
                            add_bias(b + 1, t, 2 if before else 3, (beside_bank(u, 0), beside_bank(u, 1)))
                        if before:
                            residual(b - 1, t, beside_bank(u, 2))
                            dve.sem_inc(s_s1r, 1 if behind else 3)
                    if before:
                        if (s, u) == (5, 1):
                            second_norm()
                        if s == 5 and 3 <= u < 3 + NT:
                            if u == 3:
                                dve.wait_ge(s_listed, b + 1)
                            normalise_rows(u - 3)
                        if (s, u) == (6, 1):
                            rms()
                        if (s, u) == ROUTER_AT:
                            logits(b - 1, beside_bank(u, 0))
                        if (s, u) == (7, 1):
                            shift_logits()
                        if (s, u) == (7, 5):
                            choose(b - 1)
                        if (s, u) == RANK_AT:
                            ranks(b - 1, beside_bank(u, 0))
                        if (s, u) == (7, 10):
                            weights()
                        if (s, u) == (7, 12):
                            places(b - 1)
                    elif (s, u) in (ROUTER_AT, RANK_AT):
                        dve.wait_ge(s_s1r, 3 + s1_position(b, s) + pieces_after(u))
                        dve.sem_inc(s_s1r, 3)

                def sequence(b, before, behind):
                    for s in range(PAIRS):
                        g, par = b * PAIRS + s, s % 2
                        more = s < PAIRS - 1 or behind
                        c = 0
                        for u in range(UNITS):
                            if u == 0 and more:
                                copy_k(9 + g * ROUNDS, S1[0], 1 - par, 1)
                            while more and c < pieces_after(u):
                                reduce_piece(g + 1, c)
                                c += 1
                            if u == 1 and (s or before):
                                normalise(g - 1, (s - 1) % PAIRS)
                            if u == MAX_AT and more:
                                maxima_to_rows(g + 1, 1 - par, s1_position(b, s) + beside_before(s, u) + CHUNKS)
                                if s == NT // 2 and behind:
                                    dve.sem_inc(s_qkv, 1)
                            beside(b, s, u, before, behind)
                        if s < PAIRS - 2 or behind:
                            copy_k(14 + g * ROUNDS, S1[2], par, 0)

                for half in range(2):
                    first_norm(0, half)
                    if half == 0:
                        dve.wait_ge(s_wq, 16 * 7)
                        for c in range(DC):
                            link(dve.tensor_scalar(router[:, c], router_raw[:, c], scale_raw[:, c:c + 1], None,
                                                   ALU.mult))
                    for t in range(half * HALF, (half + 1) * HALF):
                        normalise_x(0, t)
                        if t >= 1:
                            add_bias(0, t - 1, 3, S1)
                add_bias(0, NT - 1, 3, S1)
                dve.wait_ge(s_s1r, 3 + 3 * NT)
                dve.sem_inc(s_qkv, 1)
                copy_k(0, TB, 0, 0)
                copy_k(1, S1[0], 0, 1)
                for c in range(CHUNKS):
                    reduce_piece(0, c)
                maxima_to_rows(0, 0, STARTUP)
                copy_k(8, S1[2], 1, 0)
                sequences(dve, sequence)
                normalise(G - 1, PAIRS - 1)

                for t in range(NT):
                    residual(B - 1, t, S1[t % 3])
                second_norm()
                dve.wait_ge(s_listed, B + 1)
                for t in range(NT):
                    normalise_rows(t)
                rms()
                logits(B - 1, S1[0])
                shift_logits()
                choose(B - 1)
                weights()
                ranks(B - 1, S1[0])
                places(B - 1)
                end = Chain(dve, s_end, 0)
                end.link(dve.tensor_tensor(tail_f[:], running[:], e_start[:], ALU.add))
                end.link(dve.tensor_scalar(tail_index[:], tail_f[:], token[:, 0:1], -float(T), ALU.add, ALU.add))
                dve.wait_ge(s_listed, B + 2)
                end.link(dve.memset(zero_row, 0.0))
                end.link(dve.tensor_scalar(zero_row[:, D:D + 1].bitcast(I32), token[:, 0:1], 0.0, float(NOWHERE),
                                           ALU.mult, ALU.add))
                dve.sem_inc(s_tail, 1)

            @block.tensor
            def _(pe):
                pe.sem_inc(s_pv, 2)
                pe.wait_ge(s_const, 12)
                pe.wait_ge(s_dconst, 1)

                def turn(src, ready, free, n):
                    pe.wait_ge(free, n + 1)
                    for c in range(DC):
                        last = pe.transpose(TB[:, c * P:(c + 1) * P], src[:, c * P:(c + 1) * P], ident[:])
                    last.then_inc(ready, 1)

                def turn_x(b, t):
                    pe.wait_ge(s_xn, b * NT + t + 1)
                    turn(xn[:, t % 2], s_xturn, s_xcopy, b * NT + t)

                def project(b, t, position, banks):
                    pe.wait_ge(s_xcopy, 1 + b * NT + t + 1)
                    for i, (lo, hi) in enumerate(((0, 512), (512, 3 * D))):
                        pe.wait_ge(s_s1r, position + i + 1)
                        for c in range(DC):
                            last = pe.matmul(banks[i][:, 0:hi - lo], xT[:, t % 2, c], wqkv[:, c, lo:hi],
                                             start=(c == 0), stop=(c == DC - 1))
                        last.then_inc(s_qkvp, 1)

                def project_out(b, t, bank):
                    pe.wait_ge(s_acopy, 1 + (b + 1) * NT)
                    for c in range(DC):
                        last = pe.matmul(bank[:, 0:D], turned_all[:, c, t * P:(t + 1) * P], wout[:, c],
                                         start=(c == 0), stop=(c == DC - 1))
                    last.then_inc(s_proj, 1)

                def router_logits(b, bank):
                    pe.wait_ge(s_hcopy, 1 + (b + 1) * NT)
                    for t in range(NT):
                        for c in range(DC):
                            last = pe.matmul(bank[:, t * E:(t + 1) * E], turned_all[:, c, t * P:(t + 1) * P],
                                             router[:, c], start=(c == 0), stop=(c == DC - 1))
                    last.then_inc(s_logit, 1)

                def rank(b, bank):
                    pe.wait_ge(s_chosen, b + 1)
                    pe.matmul(bank[:, 0:E * NT], not_before[:], R["chosen"][:].rearrange("p e t -> p (e t)"),
                              start=True, stop=False)
                    pe.matmul(bank[:, 0:E * NT], ones[:], R["count"][:].rearrange("p e t -> p (e t)"),
                              start=False, stop=True)
                    pe.matmul(bank[:, E * NT:E * NT + E], ones[:], R["count"][:, :, NT - 1],
                              start=True, stop=True).then_inc(s_rank, 1)

                def round_(bank, src, half):
                    for i in range(HALF):
                        tile = src[:, half * HALF + i].rearrange("p j r -> p (j r)").bitcast(F32)
                        last = pe.transpose(bank[:, i * P:(i + 1) * P], tile, ident[:])
                    last.then_inc(s_round, 1)

                def scores(g, par, c, position):
                    j, qt, piece = PIECES[c]
                    lo = piece * 512
                    n = min((qt + 1) * P - lo, 512)
                    diagonal = lo + n == (qt + 1) * P
                    pe.wait_ge(s_s1r, position + 1)
                    last = pe.matmul(S1[c % 3][:, 0:n], QT[par][j][:, qt * P:(qt + 1) * P], KT[par][:, lo:lo + n],
                                     start=True, stop=not diagonal)
                    if diagonal:
                        last = pe.matmul(S1[c % 3][:, n - P:n], identb[:], mask_qk[:], start=False, stop=True)
                    last.then_inc(s_s1, 1)

                def shifted(g, par, u, copied):
                    kt, j = u // 2, u % 2
                    for n, (v, lo, hi) in enumerate(PARTS):
                        if v != u:
                            continue
                        pe.wait_ge(s_e, g * NP + n + 1)
                        if u == 0:
                            pe.wait_ge(s_q, copied - (lo == 0))
                        bank, at, end = S2[n % 3], lo % 512, (hi - 1) % 512 + 1
                        diagonal = lo == kt * P
                        last = pe.matmul(bank[:, at:end], KT[par][:, kt * P:(kt + 1) * P], QTm[par][j][:, lo:hi],
                                         start=True, stop=not diagonal)
                        if diagonal:
                            last = pe.matmul(bank[:, at:at + P], identb[:], mask_kq[:], start=False, stop=True)
                        last.then_inc(s_s2, 1)

                def values(g, par, kt):
                    pe.wait_ge(s_e, 3 + g * NP + parts_before(2 * kt + 2))
                    if kt == 0:
                        pe.wait_ge(s_o, g + 1)
                        pe.wait_ge(s_v, g + 1)
                    for h in range(2):
                        lo, hi = max(h * 512, kt * P), (h + 1) * 512
                        if lo >= hi:
                            continue
                        for j in range(2):
                            q = 32 * (2 * h + j)
                            last = pe.matmul(OB[q:q + 32, lo - h * 512:512], V[par][:, kt, j],
                                             probs[:, (2 * kt + j) % 4, lo:hi], start=(kt == 0),
                                             stop=(kt == HALF * (h + 1) - 1))
                    last.then_inc(s_pv, 1)

                def turn_output(g):
                    pe.wait_ge(s_o, 1 + g + 1)
                    for i in range(HALF):
                        last = pe.transpose(TB[:, i * P:(i + 1) * P], OT[:, i * P:(i + 1) * P], ident[:])
                    last.then_inc(s_ot, 1)

                def beside(b, s, u, before, behind, position):
                    g = b * PAIRS + s
                    if (s, u) == (0, 4) or (u == 3 and 1 <= s <= 4) or (s, u) == (6, 3):
                        pe.wait_ge(s_norm, 1 + g)
                    t = attn_turned_at(s, u)
                    if before and t is not None:
                        turn(attn[:, t], s_aturn, s_acopy, (b - 1) * NT + t)
                    t = turned_at(s, u)
                    if behind and t is not None:
                        turn_x(b + 1, t)
                    t = h_turned_at(s, u)
                    if before and t is not None:
                        if t == 0:
                            pe.wait_ge(s_h, b)
                        turn(rows[0][:, t, 0:D], s_hturn, s_hcopy, (b - 1) * NT + t)
                    t = projected_at(s, u)
                    if t is not None:
                        if behind:
                            project(b + 1, t, position, (beside_bank(u, 0), beside_bank(u, 1)))
                        if before:
                            pe.wait_ge(s_s1r, position + 3)
                            project_out(b - 1, t, beside_bank(u, 2))
                    if before and (s, u) == ROUTER_AT:
                        pe.wait_ge(s_s1r, position + 1)
                        router_logits(b - 1, beside_bank(u, 0))
                    if before and (s, u) == RANK_AT:
                        pe.wait_ge(s_s1r, position + 1)
                        rank(b - 1, beside_bank(u, 0))

                def sequence(b, before, behind):
                    for s in range(PAIRS):
                        g, par = b * PAIRS + s, s % 2
                        more = s < PAIRS - 1 or behind
                        more2 = s < PAIRS - 2 or behind
                        position = s1_position(b, s)
                        c = 0
                        for u in range(UNITS):
                            shifted(g, par, u, 6 + 4 * g if more else 4 * G)
                            if u == 0 and (s or before):
                                values(g - 1, 1 - par, NT - 1)
                            if u == 0 and more:
                                round_(S1[0], Ka, 1)
                            while more and c < pieces_after(u):
                                if c == 0:
                                    pe.wait_ge(s_k, 4 + 2 * g)
                                scores(g + 1, 1 - par, c, position + beside_before(s, u) + c)
                                c += 1
                            if u == 1 and (s or before):
                                turn_output(g - 1)
                            beside(b, s, u, before, behind, position + beside_before(s, u) + c)
                            if u in Q_AT and more2:
                                half = Q_AT.index(u)
                                if half == 0:
                                    pe.wait_ge(s_build, g + 3)
                                    pe.wait_ge(s_norm, 1 + g)
                                    if before and s == 0:
                                        pe.wait_ge(s_acopy, 1 + b * NT)
                                    if before and s == 6:
                                        pe.wait_ge(s_hcopy, 1 + b * NT)
                                else:
                                    pe.wait_ge(s_q, 6 + 4 * g + 1)
                                round_(TB, Qa[par], half)
                            if u in MAX_TURN_AT and more:
                                half = MAX_TURN_AT.index(u)
                                if half == 0:
                                    pe.wait_ge(s_m, g + 2)
                                    pe.wait_ge(s_s1r, 3 + position + beside_before(s, u) + CHUNKS)
                                round_(S1[half], Qa[1 - par], half)
                            if u % 2 and u >= 3:
                                values(g, par, u // 2 - 1)
                        if more2:
                            round_(S1[2], Ka, 0)

                pe.wait_ge(s_wq, 16 * 7)
                for t in range(NT):
                    turn_x(0, t)
                    if t >= 1:
                        project(0, t - 1, 3 * (t - 1), S1)
                project(0, NT - 1, 3 * (NT - 1), S1)
                pe.wait_ge(s_s1r, 3 + 3 * NT)
                pe.wait_ge(s_build, 1)
                round_(TB, Ka, 0)
                round_(S1[0], Ka, 1)
                round_(S1[1], Qa[0], 0)
                pe.wait_ge(s_k, 1)
                round_(TB, Qa[0], 1)
                pe.wait_ge(s_q, 2)
                pe.wait_ge(s_k, 2)
                for c in range(CHUNKS):
                    scores(0, 0, c, 3 * NT + c)
                pe.wait_ge(s_m, 1)
                for half in range(2):
                    round_(S1[half], Qa[0], half)
                pe.wait_ge(s_build, 2)
                round_(TB, Qa[1], 0)
                pe.wait_ge(s_q, 5)
                round_(TB, Qa[1], 1)
                round_(S1[2], Ka, 0)
                sequences(pe, sequence)
                values(G - 1, 1, NT - 1)
                turn_output(G - 1)

                pe.wait_ge(s_norm, 1 + G)
                for t in range(NT):
                    turn(attn[:, t], s_aturn, s_acopy, (B - 1) * NT + t)
                for t in range(NT):
                    if t >= 3:
                        pe.wait_ge(s_x2, (B - 1) * NT + t - 2)
                    project_out(B - 1, t, S1[t % 3])
                pe.wait_ge(s_h, B)
                for t in range(NT):
                    turn(rows[0][:, t, 0:D], s_hturn, s_hcopy, (B - 1) * NT + t)
                router_logits(B - 1, S1[0])
                rank(B - 1, S1[0])

        xe = rows[0]
        ye = rows[1]
        gelu_, acts, actT = (work[:, i].rearrange("p (r n) -> p r n", r=2) for i in range(3))
        gate_banks = ((S2[0], S2[1]), (S2[2], S1[2]))
        RING = 4
        assert MT % RING == 0
        q_iota = sem("step_constants"); q_table = sem("table_made"); q_tstep = sem("table_step")
        q_xe = [sem(f"expert_rows_in{r}") for r in range(RING)]
        q_out = [sem(f"expert_rows_out{r}") for r in range(RING)]
        q_xt = sem("expert_x_turned"); q_xtc = sem("expert_x_copied"); q_g = sem("gates_summed")
        q_gelu = sem("gelu_ready"); q_act = sem("act_ready"); q_at = sem("act_turned"); q_atc = sem("act_copied")
        q_dn = sem("down_summed"); q_y = sem("y_ready")

        with nc.Block() as block:

            @block.sync
            def _(sp):
                sp.wait_ge(q_table, 1)

                def load_rows(q, r):
                    row = sp.value_load(table_row[0:1, ds(q * RING + r, 1)], min_val=0, max_val=ZEROS)
                    if not isinstance(q, int):
                        sp.wait_ge(q_out[r], q * 16)
                    sp.dma_start(xe[:, r, :], routed[ds(row, P), :]).then_inc(q_xe[r], 16)

                for r in range(RING):
                    load_rows(0, r)
                with sp.Fori(1, MT // RING, 1) as q:
                    for r in range(RING):
                        load_rows(q, r)

            @block.gpsimd
            def _(pool):
                pool.iota(step_index[:], pattern=[[1, MT]], base=0, channel_multiplier=0,
                          allow_small_or_imprecise_dtypes=True).then_inc(q_iota, 1)
                pool.iota(tile_start[:], pattern=[[P, T // P]], base=0, channel_multiplier=0,
                          allow_small_or_imprecise_dtypes=True).then_inc(q_iota, 1)
                with pool.Fori(0, MT // RING, 1) as q:
                    for r in range(RING):
                        pool.wait_ge(q_y, 2 + q * RING + r + 1)
                        pool.sem_inc(s_pool_passed, 1)
                        pool.indirect_dma_start(
                            expert_out[:, :], bass.IndirectOffsetOnAxis(ap=xe[:, r, D:D + 1].bitcast(I32), axis=0),
                            ye[:, r, 0:D], None, bounds_check=TOP * T - 1, oob_is_err=False).then_inc(q_out[r], 16)
                for r in range(RING):
                    pool.wait_ge(q_out[r], 16 * (MT // RING))

            @block.scalar
            def _(act):
                act.sem_inc(q_xtc, 1)
                act.sem_inc(q_atc, 1)

                def copy_x(i, r):
                    act.wait_ge(q_xt, i + 1)
                    act.activation(xT[:, r % 2], TB[:, 0:D].rearrange("p (c m) -> p c m", c=DC),
                                   ACT.Copy).then_inc(q_xtc, 1)

                def gelu(i, r):
                    act.wait_ge(q_g, 2 * i + 1)
                    act.wait_ge(q_act, i + 1)
                    act.activation(gelu_[:, r % 2], gate_banks[r % 2][0][:, 0:HID], ACT.Gelu_apprx_tanh).then_inc(q_gelu, 1)

                def copy_act(i, r):
                    act.wait_ge(q_at, 2 + i + 1)
                    act.activation(actT[:, r % 2], OB[:, 0:HID], ACT.Copy).then_inc(q_atc, 1)

                def group(base, last):
                    for r in range(RING):
                        i = base + r
                        copy_act(i, r)
                        if not (last and r == RING - 1):
                            gelu(i + 1, r + 1)
                        if not (last and r >= RING - 2):
                            copy_x(i + 2, r)

                copy_x(0, 0)
                gelu(0, 0)
                copy_x(1, 1)
                with act.Fori(0, MT // RING - 1, 1) as q:
                    group(q * RING, False)
                group(MT - RING, True)

            @block.vector
            def _(dve):
                dve.sem_inc(q_act, 2)
                dve.sem_inc(q_y, 2)
                chain = Chain(dve, q_tstep, 0)
                link = chain.link
                most = T // P
                big = work[0:1].rearrange("p a n -> p (a n)")
                sizes = big[:, 0:E * most].rearrange("p (e j) -> p e j", e=E)
                reached_end = big[:, E * most + MT * E:]
                reached = big[:, E * most:E * most + MT * E].rearrange("p (s e) -> p s e", e=E)
                weighed = reached_end[:, 0:MT * E].rearrange("p (s e) -> p s e", e=E)
                small = xin[0:1].rearrange("p t d -> p (t d)")
                tiles, ends = small[:, 0:E], small[:, E:2 * E]
                count, which, first, local = (small[:, 64 + n * MT:64 + (n + 1) * MT] for n in range(4))
                dve.wait_ge(q_iota, 2)
                link(dve.tensor_tensor(sizes, running[0:1].unsqueeze(2).to_broadcast([1, E, most]),
                                       tile_start[:].unsqueeze(1).to_broadcast([1, E, most]), ALU.is_gt))
                link(dve.tensor_reduce(tiles, sizes, AX.X, ALU.add))
                link(dve.tensor_tensor_scan(ends, ones[0:1, 0:E], tiles, 0.0, ALU.mult, ALU.add))
                link(dve.tensor_tensor(reached, step_index[:].unsqueeze(2).to_broadcast([1, MT, E]),
                                       ends.unsqueeze(1).to_broadcast([1, MT, E]), ALU.is_ge))
                link(dve.tensor_reduce(which, reached, AX.X, ALU.add))
                link(dve.tensor_tensor(weighed, reached, tiles.unsqueeze(1).to_broadcast([1, MT, E]), ALU.mult))
                link(dve.tensor_reduce(first, weighed, AX.X, ALU.add))
                link(dve.tensor_tensor(local, step_index[:], first, ALU.subtract))
                link(dve.tensor_scalar(count, which, float(E), float(P), ALU.is_lt, ALU.mult))
                link(dve.tensor_tensor(local, local, count, ALU.mult))
                link(dve.scalar_tensor_tensor(out=table_row[:], in0=which, scalar=float(REGION), in1=local,
                                              op0=ALU.mult, op1=ALU.add))
                link(dve.tensor_scalar(table_expert[:], which, float(E - 1), None, ALU.min))
                dve.sem_inc(q_table, 1)

                def multiply(i, r):
                    dve.wait_ge(q_gelu, i + 1)
                    dve.wait_ge(q_g, 2 * i + 2)
                    dve.wait_ge(q_at, i + 1)
                    dve.tensor_tensor(acts[:, r % 2], gelu_[:, r % 2], gate_banks[r % 2][1][:, 0:HID],
                                      ALU.mult).then_inc(q_act, 1)

                def weigh(i, q, r):
                    dve.wait_ge(q_dn, i + 1)
                    if q is not None:
                        dve.wait_ge(q_out[r], q * 16)
                    dve.tensor_scalar(ye[:, r, 0:D], S1[r % 2][:, 0:D], xe[:, r, D + 1:D + 2], None,
                                      ALU.mult).then_inc(q_y, 1)

                def group(q, base, last):
                    for r in range(RING):
                        if not (last and r == RING - 1):
                            multiply(base + r + 1, r + 1)
                        weigh(base + r, q, r)

                multiply(0, 0)
                group(None, 0, False)
                with dve.Fori(1, MT // RING - 1, 1) as q:
                    group(q, q * RING, False)
                group(MT // RING - 1, MT - RING, True)

            @block.tensor
            def _(pe):
                pe.sem_inc(q_at, 2)
                pe.wait_ge(q_table, 1)

                def expert(i):
                    return pe.value_load(table_expert[0:1, ds(i, 1)], min_val=0, max_val=E - 1)

                def turn_x(i, q, r):
                    pe.wait_ge(q_xe[r], 16 * (q + 1))
                    pe.wait_ge(q_xtc, i + 1)
                    for c in range(DC):
                        last = pe.transpose(TB[:, c * P:(c + 1) * P], xe[:, r, c * P:(c + 1) * P], ident[:])
                    last.then_inc(q_xt, 1)

                def gates(i, r, n):
                    e = expert(i)
                    pe.wait_ge(q_xtc, 1 + i + 1)
                    pe.wait_ge(q_act, i + 1)
                    for c in range(DC):
                        w = wg[c][:, ds(e, 1), n * HID:(n + 1) * HID].rearrange("p a h -> p (a h)")
                        last = pe.matmul(gate_banks[r % 2][n][:, 0:HID], xT[:, r % 2, c], w,
                                         start=(c == 0), stop=(c == DC - 1))
                    last.then_inc(q_g, 1)

                def turn_act(i, r):
                    pe.wait_ge(q_act, 2 + i + 1)
                    pe.wait_ge(q_atc, i + 1)
                    for c in range(HC):
                        last = pe.transpose(OB[:, c * P:(c + 1) * P], acts[:, r % 2, c * P:(c + 1) * P], ident[:])
                    last.then_inc(q_at, 1)

                def down(i, r):
                    e = expert(i)
                    pe.wait_ge(q_atc, 1 + i + 1)
                    pe.wait_ge(q_y, i + 1)
                    for c in range(HC):
                        w = wl[:, c, ds(e, 1), :].rearrange("p a d -> p (a d)")
                        last = pe.matmul(S1[r % 2][:, 0:D], actT[:, r % 2, c * P:(c + 1) * P], w,
                                         start=(c == 0), stop=(c == HC - 1))
                    last.then_inc(q_dn, 1)

                def group(q, base, last):
                    for r in range(RING):
                        i = base + r
                        if not (last and r == RING - 1):
                            gates(i + 1, r + 1, 0)
                        turn_act(i, r)
                        if not (last and r == RING - 1):
                            gates(i + 1, r + 1, 1)
                        if not (last and r >= RING - 2):
                            turn_x(i + 2, q + (r + 2) // RING, (r + 2) % RING)
                        down(i, r)

                turn_x(0, 0, 0)
                pe.wait_ge(s_wg, 16 * WEIGHT_LOADS)
                gates(0, 0, 0)
                gates(0, 0, 1)
                turn_x(1, 0, 1)
                with pe.Fori(0, MT // RING - 1, 1) as q:
                    group(q, q * RING, False)
                group(MT // RING - 1, MT - RING, True)

        f_in = [sem(f"final_in{i}") for i in range(2)]
        f_out = [sem(f"final_out{i}") for i in range(2)]
        f_step = sem("final_step")
        f_done = [sem(f"final_done{i}") for i in range(2)]
        parts = [[shared[:, n * NT * D:(n + 1) * NT * D] for n in (2 * i, 2 * i + 1)] for i in range(3)]
        assert B % 2 == 0

        def tiled(v):
            return v.rearrange("p (t d) -> p t d", t=NT)

        with nc.Block() as block:

            @block.sync
            def _(sp):
                with sp.Fori(0, B // 2, 1) as i:
                    for m in range(2):
                        b = 2 * i + m
                        sp.wait_ge(f_out[m], 1 + i * 16)
                        for n, src in enumerate((x2_rows[b], expert_rows[0, b], expert_rows[1, b])):
                            sp.dma_start(tiled(parts[n][m]), src).then_inc(f_in[m], 16)

            @block.vector
            def _(dve):
                with dve.Fori(0, B // 2, 1) as i:
                    for m in range(2):
                        dve.wait_ge(f_in[m], (i + 1) * 48)
                        dve.tensor_tensor(parts[0][m], parts[0][m], parts[1][m], ALU.add).then_inc(f_step, 1)
                        dve.wait_ge(f_step, 2 * i + m + 1)
                        dve.tensor_tensor(parts[0][m], parts[0][m], parts[2][m], ALU.add).then_inc(f_done[m], 1)

            @block.scalar
            def _(act):
                for m in range(2):
                    act.sem_inc(f_out[m], 1)
                with act.Fori(0, B // 2, 1) as i:
                    for m in range(2):
                        act.wait_ge(f_done[m], i + 1)
                        act.dma_start(out_rows[2 * i + m], tiled(parts[0][m])).then_inc(f_out[m], 16)
                for m in range(2):
                    act.wait_ge(f_out[m], 1 + 16 * (B // 2))


def kernel(L0_attn_x, L0_attn_qkv_w, L0_attn_qkv_b, L0_attn_out_w, L0_attn_out_b, L0_ffn_router_scale,
           L0_ffn_router_w, L0_ffn_gating_w, L0_ffn_linear_w, L0_ffn_per_expert_scale):
    import numpy as np
    import concourse.bacc as bacc
    from concourse.bass_utils import run_bass_kernel_spmd

    nc = bacc.Bacc("TRN2", target_bir_lowering=False, num_devices=1)
    given = {"x": L0_attn_x, "qkv_w": L0_attn_qkv_w, "qkv_b": L0_attn_qkv_b, "out_w": L0_attn_out_w,
             "out_b": L0_attn_out_b, "router_scale": L0_ffn_router_scale, "router_w": L0_ffn_router_w,
             "gate_w": np.transpose(np.asarray(L0_ffn_gating_w), (3, 0, 1, 2)), "linear_w": L0_ffn_linear_w,
             "expert_scale": L0_ffn_per_expert_scale}
    arrays, args = {}, []
    for name, value in given.items():
        a = np.ascontiguousarray(value)
        arrays[name] = a
        args.append(nc.dram_tensor(name, a.shape, mybir.dt.from_np(a.dtype), kind="ExternalInput").ap())
    shape = arrays["x"].shape
    args.append(nc.dram_tensor("out", shape, F32, kind="ExternalOutput").ap())
    preln_attention_then_routed_ffn(nc, *args)
    return run_bass_kernel_spmd(nc, [arrays], core_ids=[0]).results[0]["out"]
```

```python
import concourse.bass as bass
from concourse import mybir
from contextlib import ExitStack

F32 = mybir.dt.float32
F32R = mybir.dt.float32r
BF16 = mybir.dt.bfloat16
I32 = mybir.dt.int32
ALU = mybir.AluOpType
ACT = mybir.ActivationFunctionType
AX = mybir.AxisListType
ds = bass.ds

P = 128
HEADS = 16
HD = 16
D = HEADS * HD
ROWS = 64
PRODUCTS = 3 * HD
SCORED = PRODUCTS + 2
E = 8
TOP = 2
MASKED = -1e30
LOWEST = -3e38
RSQRT_MAGIC = 0x5F3759DF
ROW = D + 2


class Chain:

    def __init__(self, engine, sem, per_round, fixed=0):
        self.engine, self.sem, self.per_round, self.n, self.fixed = engine, sem, per_round, 0, fixed
        self.base = fixed

    def begin(self, round_):
        self.base, self.n = round_ * self.per_round + self.fixed, 0

    def link(self, instruction):
        self.n += 1
        instruction.then_inc(self.sem, 1)
        self.engine.wait_ge(self.sem, self.base + self.n)

    def step(self, instruction):
        if self.n:
            self.engine.wait_ge(self.sem, self.base + self.n)
        self.n += 1
        instruction().then_inc(self.sem, 1)

    def settle(self):
        self.engine.wait_ge(self.sem, self.base + self.n)

    def end(self):
        assert self.n == self.per_round, (self.n, self.per_round)


def preln_attention_then_routed_ffn(
    nc: bass.Bass,
    x: bass.AP,
    qkv_w: bass.AP,
    qkv_b: bass.AP,
    out_w: bass.AP,
    out_b: bass.AP,
    router_scale: bass.AP,
    router_w: bass.AP,
    gate_w: bass.AP,
    linear_w: bass.AP,
    expert_scale: bass.AP,
    out: bass.AP,
):
    B, S, _ = x.shape
    HID = linear_w.shape[1]
    T = B * S
    NT = S // P
    HALF = NT // 2
    HC = HID // P
    DC = D // P
    PAIRS = HEADS // 2
    REGION = T + P
    ZEROS = E * REGION
    MT = TOP * T // P + E
    AHEAD = 2
    UNITS = 2 * NT
    CHUNKS = 2 * (HALF + 2 * (NT - HALF))
    ROUNDS = 6
    BR = PAIRS * ROUNDS

    x_rows = x.rearrange("b (t p) d -> b p t d", p=P)
    sums = nc.dram_tensor("sums", [T + P, D], F32, kind="Internal").ap()
    x2_rows = sums[0:T].rearrange("(b t p) d -> b p t d", b=B, p=P)
    routed = nc.dram_tensor("routed", [ZEROS + P, ROW], F32, kind="Internal").ap()

    with ExitStack() as ctx:
        def sb(name, shape, dt=F32):
            return ctx.enter_context(nc.sbuf_tensor(name, shape, dt))

        def sem(name):
            return ctx.enter_context(nc.semaphore(name))

        TILES = NT * D
        shared = sb("shared", [P, 12 * TILES])
        qkv_all = shared[:, 0:2 * NT * 3 * D].rearrange("p (t n) -> p t n", n=3 * D)
        attn = shared[:, NT * 6 * D:NT * 7 * D].rearrange("p (t n) -> p t n", t=NT)
        turned_all = shared[:, NT * 7 * D:NT * 8 * D].rearrange("p (c s) -> p c s", c=DC)
        probs = shared[:, 8 * TILES:10 * TILES].rearrange("p (n s) -> p n s", s=S)
        xres = shared[:, 10 * TILES:11 * TILES].rearrange("p (t d) -> p t d", t=NT)
        wqkv = shared[:, 11 * TILES:11 * TILES + DC * 3 * D].rearrange("p (c n) -> p c n", c=DC)
        wout = shared[:, 12 * TILES - DC * D:12 * TILES].rearrange("p (c n) -> p c n", c=DC)
        wg = [shared[:, c * E * 2 * HID:(c + 1) * E * 2 * HID].rearrange("p (e n) -> p e n", e=E) for c in range(DC)]
        wl = shared[:, DC * E * 2 * HID:].rearrange("p (c e d) -> p c e d", c=HC, e=E)
        assert DC == 2 and HC == 4 and 4 * S == 2 * TILES and E * 2 * HID == 4 * TILES and E * D == TILES
        assert DC * 4 * D == TILES and B % 2 == 0
        qkv_bias = sb("qkv_bias", [P, 3 * D])
        out_bias = sb("out_bias", [P, D])
        xin = sb("xin", [P, HALF, D])
        xn = sb("xn", [P, 2, D])
        xT = sb("xT", [P, DC, 2, P])
        Qa = [sb(f"Qa{i}", [P, NT, 2, ROWS], F32R) for i in range(2)]
        Ka = sb("Ka", [P, NT, 2, ROWS], F32R)
        V = [sb(f"V{i}", [P, NT, 2, 32]) for i in range(2)]
        KT = [sb(f"KT{i}", [P, S], F32R) for i in range(2)]
        QT = [[sb(f"QT{i}_{j}", [P, S], F32R) for j in range(2)] for i in range(2)]
        QTm = [[sb(f"QTm{i}_{j}", [P, S], F32R) for j in range(2)] for i in range(2)]
        OT = sb("OT", [P, 4 * P])
        work = sb("work", [P, 3, 2 * HID])
        rows = [sb(f"rows{k}", [P, NT, ROW]) for k in range(TOP)]
        ident = sb("ident", [P, P])
        identb = sb("identb", [P, P], BF16)
        mask_qk = sb("mask_qk", [P, P], BF16)
        mask_kq = sb("mask_kq", [P, P], BF16)
        not_before = sb("not_before", [P, P])
        ones = sb("ones", [P, P])
        maxima = sb("maxima", [P, 2, NT, 2])
        top_score = sb("top_score", [P, 2, NT])
        rden = sb("rden", [P, HALF, 4])
        scale_raw = sb("scale_raw", [P, DC])
        router_raw = sb("router_raw", [P, DC, E])
        router = sb("router", [P, DC, E])
        escale = sb("escale", [P, E])
        e_index = sb("e_index", [P, E, NT])
        e_start = sb("e_start", [P, E])
        same_expert = sb("same_expert", [P, E, NT])
        token = sb("token", [P, NT])
        running = sb("running", [P, E])
        norm1 = {n: sb("n1_" + n, [P, HALF] + w) for n, w in
                 (("stats", [6]), ("moments", [2]), ("var", []), ("rstd", []), ("newton", []))}
        norm2 = {n: sb("n2_" + n, [P, NT] + w) for n, w in
                 (("stats", [6]), ("moments", [2]), ("var", []), ("rstd", []), ("newton", []))}
        rnorm = {n: sb("rn_" + n, [P, NT]) for n in ("var", "rstd", "newton")}
        R = {n: sb("r_" + n, [P, E, NT]) for n in
             ("logits", "left", "pick0", "pick1", "chosen", "count", "slot", "exps", "work")}
        V1 = {n: sb("v_" + n, [P, NT]) for n in ("best", "index", "sum", "rsum", "gate", "flag", "w", "dest")}
        slot_index = [sb(f"slot_index{k}", [P, NT], I32) for k in range(TOP)]
        zero_row = sb("zero_row", [P, ROW])
        tail_f = sb("tail_f", [P, E])
        tail_index = sb("tail_index", [P, E], I32)
        table_row = sb("table_row", [1, MT], I32)
        table_expert = sb("table_expert", [1, MT], I32)
        step_index = sb("step_index", [1, MT])
        tile_start = sb("tile_start", [1, T // P])

        def pb(name, n):
            return ctx.enter_context(nc.psum_tensor(name, [P, n], F32))
        S2 = [pb(f"S2_{i}", 512) for i in range(3)]
        S1 = [pb(f"S1_{i}", 512) for i in range(3)]
        TB = pb("TB", 512)
        OB = pb("OB", 512)

        s_wq = sem("weights_in"); s_wg = sem("gate_weights_in")
        s_const = sem("constants_made"); s_dconst = sem("vector_constants")
        s_x = sem("x_in"); s_res = sem("residual_in"); s_resb = sem("residual_biased")
        s_xn = sem("xn_ready"); s_xturn = sem("x_turned"); s_xcopy = sem("x_turned_copied")
        s_aturn = sem("attn_turned"); s_acopy = sem("attn_turned_copied")
        s_hturn = sem("h_turned"); s_hcopy = sem("h_turned_copied")
        s_qkvp = sem("qkv_summed"); s_qkv = sem("qkv_ready")
        s_build = sem("qk_rows_built"); s_v = sem("v_built"); s_pool = sem("pool_step"); s_set = sem("pool_setup")
        s_round = sem("round_turned"); s_q = sem("q_copied"); s_k = sem("k_copied")
        s_qm = sem("q_max_copied"); s_h1 = sem("h_copied"); s_listed = sem("rows_in_lists")
        s_s1 = sem("scores_ready"); s_s1r = sem("s1_banks_read"); s_m = sem("maxima_in_rows"); s_mstep = sem("max_step")
        s_s2 = sem("shifted_scores_ready"); s_e = sem("probs_ready"); s_pv = sem("pv_done")
        s_o = sem("o_copied"); s_ot = sem("o_turned"); s_norm = sem("o_normalised"); s_nstep = sem("norm_step")
        s_proj = sem("projected"); s_x2 = sem("x2_ready"); s_h = sem("h_ready"); s_logit = sem("logits_summed")
        s_soft = sem("router_shifted"); s_softed = sem("router_exps")
        s_chosen = sem("chosen_ready"); s_rank = sem("ranks_summed"); s_slot = sem("slots_ready")
        s_scat = sem("rows_scattered"); s_x2out = sem("x2_stored"); s_link1 = sem("norm1_step")
        s_link2 = sem("norm2_step"); s_setup = sem("vector_setup"); s_end = sem("vector_end")
        s_pool_passed = sem("pool_waits_passed"); s_dve_passed = sem("vector_waits_passed")
        s_tail = sem("tail_ready"); s_tailout = sem("zero_rows_stored"); s_ends = sem("list_ends_zeroed")

        PIECES = [(j, qt, piece) for qt in reversed(range(NT)) for j in range(2) for piece in range(1 if qt < HALF else 2)]
        SCORE_UNITS = range(1, UNITS - 4)

        QKV_HALVES = ((0, 512), (512, 3 * D))
        FIRST_USES = 2 * NT + 2
        STARTUP = FIRST_USES + CHUNKS
        assert STARTUP % 3 == 0
        PARTS = [(u, max(h * 512, u // 2 * P), (h + 1) * 512) for u in range(UNITS)
                 for h in range(0 if u // 2 < HALF else 1, 2)]
        NP = len(PARTS)
        assert NP % 3 == 0 and CHUNKS % 3 == 0

        def parts_before(u):
            return sum(1 for v, _, _ in PARTS if v < u)

        def beside_before(s, u):
            return sum(1 if projected_at(s, v) else 3 * ((s, v) in (ROUTER_AT, RANK_AT)) for v in range(u))

        def beside_bank(s, u):
            return S1[(beside_before(s, u) + pieces_after(u)) % 3]

        def s1_position(b, s):
            return STARTUP + b * (PAIRS * CHUNKS + 3 * (NT + 2)) + s * CHUNKS + 3 * (
                2 * min(max(s - 1, 0), NT // 2) + (s > 6))

        def piece_keys(c):
            j, qt, piece = PIECES[c]
            return min((qt + 1) * P - piece * 512, 512)

        def pieces_after(u):
            unit_columns = [S - v // 2 * P for v in SCORE_UNITS]
            share = sum(n for v, n in zip(SCORE_UNITS, unit_columns) if v <= u) / sum(unit_columns)
            total, c, reached = sum(piece_keys(c) for c in range(CHUNKS)), 0, 0
            while c < CHUNKS and reached < share * total:
                reached += piece_keys(c)
                c += 1
            return c

        def projected_at(s, u):
            return (2 * (s - 1) + (u - 4) // 3, (u - 4) % 3) if 1 <= s <= NT // 2 and 4 <= u < 10 else None

        def turned_at(s, u):
            return s - 1 if 1 <= s <= NT // 2 and u == 3 else None

        def attn_turned_at(s, u):
            return u - 4 if s == 0 and 4 <= u < 4 + HALF else None

        def h_turned_at(s, u):
            return u - 3 if s == 6 and 3 <= u < 3 + HALF else None

        ROUTER_AT, RANK_AT = (6, 11), (7, 9)
        MAX_AT, MAX_TURN_AT = {9: 1, 12: 0}, {12: 1, 14: 0}
        LATER_PIECES = sum(qt >= HALF for _, qt, _ in PIECES)
        Q_AT = (7, 9)
        assert pieces_after(min(MAX_AT)) >= LATER_PIECES
        assert UNITS == 16
        assert len(PIECES) == CHUNKS and PAIRS == 8 and NT == 8
        G = B * PAIRS
        RSQRT_LINKS = 11
        NORM_STEPS = 2 + RSQRT_LINKS
        FIRST_STEPS = HALF + 1 + RSQRT_LINKS
        ROUTE_LINKS = (NT + (NT + 1 + RSQRT_LINKS) + (3 + RSQRT_LINKS + 1)
                       + 1 + 2 + 5 + 5 + 2 + 10 + 3 + TOP * 5 + 1)
        WEIGHT_LOADS = 4 + HC

        def sequences(engine, sequence):
            sequence(0, False, True)
            with engine.Fori(1, B - 1, 1) as b:
                sequence(b, True, True)
            sequence(B - 1, True, False)

        with nc.Block() as block:

            @block.sync
            def _(sp):
                sp.dma_start(xin[:], x_rows[0, :, 0:HALF]).then_inc(s_x, 16)
                sp.dma_start(xres[:], x_rows[0]).then_inc(s_res, 16)
                sp.dma_start(wqkv[:], qkv_w.rearrange("(c p) n -> p c n", p=P)).then_inc(s_wq, 16)
                sp.dma_start(qkv_bias[:], qkv_b.partition_broadcast(P)).then_inc(s_wq, 16)
                sp.dma_start(wout[:], out_w.rearrange("(c p) n -> p c n", p=P)).then_inc(s_wq, 16)
                sp.dma_start(out_bias[:], out_b.partition_broadcast(P)).then_inc(s_wq, 16)
                sp.dma_start(scale_raw[:], router_scale.rearrange("(c p) -> p c", p=P),
                             allow_slow_non_contiguous=True).then_inc(s_wq, 16)
                sp.dma_start(router_raw[:], router_w.rearrange("(c p) e -> p c e", p=P)).then_inc(s_wq, 16)
                sp.dma_start(escale[:], expert_scale.partition_broadcast(P)).then_inc(s_wq, 16)

                def load_x(b, half):
                    sp.wait_ge(s_xn, b * NT + half * HALF)
                    sp.dma_start(xin[:], x_rows[b, :, half * HALF:(half + 1) * HALF]).then_inc(s_x, 16)

                def residual(b):
                    sp.dma_start(xres[:], x_rows[b]).then_inc(s_res, 16)

                def store(b):
                    sp.wait_ge(s_x2, (b + 1) * NT)
                    sp.dma_start(x2_rows[b], xres[:]).then_inc(s_x2out, 16)
                    sp.wait_ge(s_x2out, (b + 1) * 16)
                    sp.wait_ge(s_h, (b + 1) * NT)

                def sequence(b, before, behind):
                    if behind:
                        load_x(b + 1, 0)
                        load_x(b + 1, 1)
                    if before:
                        store(b - 1)
                        residual(b)

                def load_gates(c, first, last):
                    sp.dma_start(wg[c][:, first:last],
                                 gate_w[c * P:(c + 1) * P, first:last].rearrange("p e g h -> p e (g h)"))\
                        .then_inc(s_wg, 16)

                def load_linear(c):
                    sp.dma_start(wl[:, c], linear_w[:, c * P:(c + 1) * P, :].rearrange("e p d -> p e d"))\
                        .then_inc(s_wg, 16)

                sequence(0, False, True)
                with sp.Fori(1, B - 1, 1) as b:
                    sequence(b, True, True)
                sp.wait_ge(s_build, (B - 1) * PAIRS)
                sp.wait_ge(s_v, (B - 1) * PAIRS)
                load_gates(0, 0, 6)
                sequence(B - 1, True, False)
                sp.wait_ge(s_build, G)
                sp.wait_ge(s_v, G)
                load_gates(0, 6, 8)
                load_gates(1, 0, 4)
                sp.wait_ge(s_pv, 2 + G * NT)
                load_linear(0)
                load_linear(1)
                sp.wait_ge(s_proj, B * NT)
                load_linear(3)
                store(B - 1)
                load_linear(2)
                sp.wait_ge(s_logit, B)
                load_gates(1, 4, 8)
                sp.wait_ge(s_tail, 1)
                for e in range(E):
                    row = sp.value_load(tail_index[0:1, e:e + 1], min_val=0, max_val=ZEROS - P)
                    sp.dma_start(routed[ds(row, P), :], zero_row[:]).then_inc(s_ends, 16)
                sp.wait_ge(s_ends, 16 * E)

            @block.gpsimd
            def _(pool):
                chain = Chain(pool, s_set, 0)
                link = chain.link
                link(pool.memset(ident[:], 0.0))
                pool.affine_select(out=ident[:], in_=ident[:], compare_op=ALU.not_equal, fill=1.0, base=0,
                                   pattern=[[-1, P]], channel_multiplier=1).then_inc(s_const, 1)
                link(pool.memset(identb[:], 0.0))
                pool.affine_select(out=identb[:], in_=identb[:], compare_op=ALU.not_equal, fill=1.0, base=0,
                                   pattern=[[-1, P]], channel_multiplier=1).then_inc(s_const, 1)
                link(pool.memset(mask_qk[:], 0.0))
                pool.affine_select(out=mask_qk[:], in_=mask_qk[:], compare_op=ALU.is_ge, fill=MASKED, base=0,
                                   pattern=[[-1, P]], channel_multiplier=1).then_inc(s_const, 1)
                link(pool.memset(mask_kq[:], 0.0))
                pool.affine_select(out=mask_kq[:], in_=mask_kq[:], compare_op=ALU.is_ge, fill=MASKED, base=0,
                                   pattern=[[1, P]], channel_multiplier=-1).then_inc(s_const, 1)
                link(pool.memset(not_before[:], 0.0))
                pool.affine_select(out=not_before[:], in_=not_before[:], compare_op=ALU.is_gt, fill=-1.0, base=0,
                                   pattern=[[1, P]], channel_multiplier=-1).then_inc(s_const, 1)
                pool.memset(ones[:], 1.0).then_inc(s_const, 1)
                pool.iota(e_index[:], pattern=[[1, E], [0, NT]], base=0, channel_multiplier=0,
                          allow_small_or_imprecise_dtypes=True).then_inc(s_const, 1)
                pool.iota(token[:], pattern=[[P, NT]], base=0, channel_multiplier=1,
                          allow_small_or_imprecise_dtypes=True).then_inc(s_const, 1)
                pool.iota(step_index[:], pattern=[[1, MT]], base=0, channel_multiplier=0,
                          allow_small_or_imprecise_dtypes=True).then_inc(s_const, 1)
                pool.iota(tile_start[:], pattern=[[P, T // P]], base=0, channel_multiplier=0,
                          allow_small_or_imprecise_dtypes=True).then_inc(s_const, 1)
                pool.memset(zero_row[:], 0.0).then_inc(s_const, 1)
                for i in range(2):
                    pool.memset(V[i][:], 0.0).then_inc(s_const, 1)
                pool.wait_ge(s_const, 13)
                for i in range(2):
                    pool.memset(V[i][:, :, :, HD:HD + 1], 1.0).then_inc(s_const, 1)
                pool.wait_ge(s_dconst, 1)
                pool.dma_start(routed[ZEROS:ZEROS + P, :], zero_row[:]).then_inc(s_tailout, 16)
                pool.dma_start(sums[T:T + P, :], zero_row[:, 0:D]).then_inc(s_tailout, 16)

                def hold(semaphore, value):
                    pool.wait_ge(semaphore, value)
                    pool.sem_inc(s_pool_passed, 1)

                def of_pair(b, which, s):
                    tiles = qkv_all[:, ds(b % 2 * NT, NT), which * D + s * 2 * HD:which * D + (s + 1) * 2 * HD]
                    return tiles.rearrange("p t (j d) -> p t j d", j=2)

                def build_qk(g, b, s, par):
                    for n, (dst, which, hi, lo) in enumerate(((Qa[par], 0, (0, 1), 2), (Ka, 1, (0, 2), 1))):
                        src = of_pair(b, which, s)
                        for m in hi:
                            pool.tensor_copy(dst[:, :, :, m * HD:(m + 1) * HD], src).then_inc(s_pool, 1)
                        if n == 0:
                            pool.memset(dst[:, :, :, PRODUCTS:SCORED].bitcast(F32), 0.0).then_inc(s_pool, 1)
                        hold(s_pool, g * 5 + (3 if n == 0 else 5))
                        last = pool.tensor_tensor(dst[:, :, :, lo * HD:(lo + 1) * HD], src,
                                                  dst[:, :, :, 0:HD].bitcast(F32), ALU.subtract)
                    last.then_inc(s_build, 1)

                def build_v(b, s, par):
                    pool.tensor_copy(V[par][:, :, :, 0:HD], of_pair(b, 2, s)).then_inc(s_v, 1)

                def scatter(t, choices=range(TOP)):
                    for k in choices:
                        pool.indirect_dma_start(
                            routed[:, :], bass.IndirectOffsetOnAxis(ap=slot_index[k][:, t:t + 1], axis=0),
                            rows[k][:, t, :], None).then_inc(s_scat, 16)

                def copy_rows(b):
                    hold(s_h, (b + 1) * NT)
                    pool.tensor_copy(rows[1][:, :, 0:D], rows[0][:, :, 0:D]).then_inc(s_h1, 1)

                def bias_residual(b):
                    hold(s_res, (b + 1) * 16)
                    pool.tensor_tensor(xres[:], xres[:], out_bias[:].unsqueeze(1).to_broadcast([P, NT, D]),
                                       ALU.add).then_inc(s_resb, 1)

                def slot(b, s, before, behind):
                    g, par = b * PAIRS + s, s % 2
                    if s < PAIRS - 2 or behind:
                        b2, s2 = (b, s + 2) if s < PAIRS - 2 else (b + 1, s + 2 - PAIRS)
                        if s == PAIRS - 2:
                            hold(s_qkv, b + 2)
                        hold(s_round, g * ROUNDS + 10)
                        build_qk(g + 2, b2, s2, par)
                    if s < PAIRS - 1 or behind:
                        b1, s1 = (b, s + 1) if s < PAIRS - 1 else (b + 1, 0)
                        hold(s_pv, 2 + g * NT)
                        build_v(b1, s1, 1 - par)
                    if before and s == 0:
                        bias_residual(b - 1)

                def sequence(b, before, behind, routed_before):
                    for s in range(PAIRS):
                        slot(b, s, before, behind)
                        if s < NT // 2 and routed_before:
                            if s == 0:
                                hold(s_slot, (b - 1) * TOP)
                                hold(s_h1, b - 1)
                            scatter(2 * s)
                            scatter(2 * s + 1)
                        if s == NT // 2 and before:
                            if routed_before:
                                hold(s_scat, (b - 1) * 16 * TOP * NT)
                            pool.sem_inc(s_listed, 1)
                        if s == 6 and before:
                            copy_rows(b - 1)

                hold(s_qkv, 1)
                build_qk(0, 0, 0, 0)
                build_v(0, 0, 0)
                hold(s_round, 2)
                build_qk(1, 0, 1, 1)
                sequence(0, False, True, False)
                sequence(1, True, True, False)
                with pool.Fori(2, B - 1, 1) as b:
                    sequence(b, True, True, True)
                sequence(B - 1, True, False, True)
                bias_residual(B - 1)
                hold(s_slot, (B - 1) * TOP)
                hold(s_h1, B - 1)
                for t in range(NT):
                    scatter(t)
                hold(s_scat, (B - 1) * 16 * TOP * NT)
                pool.sem_inc(s_listed, 1)
                copy_rows(B - 1)
                for k in range(TOP):
                    hold(s_slot, (B - 1) * TOP + k + 1)
                    if k == 1:
                        hold(s_h1, B)
                    for t in range(NT):
                        scatter(t, (k,))
                pool.wait_ge(s_scat, B * 16 * TOP * NT)
                pool.wait_ge(s_tailout, 16 * 2)

            @block.scalar
            def _(act):
                act.sem_inc(s_xcopy, 1)
                act.sem_inc(s_acopy, 1)
                act.sem_inc(s_hcopy, 1)
                act.sem_inc(s_e, 3)
                act.sem_inc(s_o, 1)
                turned = TB[:].rearrange("p (c n) -> p c n", c=DC)

                def copy_x(b, m):
                    act.wait_ge(s_xturn, b * HALF + m + 1)
                    act.activation(xT[:].rearrange("p c r n -> p c (r n)"), turned, ACT.Copy).then_inc(s_xcopy, 1)

                def copy_to_all(b, m, ready, copied):
                    act.wait_ge(ready, b * HALF + m + 1)
                    act.activation(turned_all[:, :, m * 2 * P:(m + 1) * 2 * P], turned, ACT.Copy).then_inc(copied, 1)

                def copy_q(n, bank, dst, half, heads=(0, 1)):
                    act.wait_ge(s_round, n + 1)
                    for j in heads:
                        r = slice(j * ROWS, (j + 1) * ROWS)
                        last = act.activation(dst[j][r, half * 512:(half + 1) * 512], bank[r, :], ACT.Copy)
                    last.then_inc(s_q, 1)

                def exps(g, u):
                    kt = u // 2
                    act.wait_ge(s_pv, g * NT + kt + 1)
                    for n, (v, lo, hi) in enumerate(PARTS):
                        if v == u:
                            act.wait_ge(s_s2, g * NP + n + 1)
                            act.activation(probs[:, u % 4, lo:hi], S2[n % 3][:, lo % 512:(hi - 1) % 512 + 1],
                                           ACT.Exp, scale=float(HD) ** -0.5).then_inc(s_e, 1)

                def copy_o(g):
                    act.wait_ge(s_pv, 2 + (g + 1) * NT)
                    act.activation(OT[:], OB[:], ACT.Copy).then_inc(s_o, 1)

                def sequence(b, before, behind):
                    for s in range(PAIRS):
                        g = b * PAIRS + s
                        for u in range(UNITS):
                            exps(g, u)
                            if before and attn_turned_at(s, u) is not None:
                                copy_to_all(b - 1, attn_turned_at(s, u), s_aturn, s_acopy)
                            if before and h_turned_at(s, u) is not None:
                                copy_to_all(b - 1, h_turned_at(s, u), s_hturn, s_hcopy)
                            if behind and turned_at(s, u) is not None:
                                copy_x(b + 1, turned_at(s, u))
                            if before and (s, u) == (6, 13):
                                router_exps(b - 1)
                            if u == 0 and (s or before):
                                copy_o(g - 1)
                            if u in Q_AT and (s < PAIRS - 2 or behind):
                                half = Q_AT.index(u)
                                copy_q(10 + g * ROUNDS + half, TB, QT[s % 2], half)
                            if u in MAX_TURN_AT and (s < PAIRS - 1 or behind):
                                half = MAX_TURN_AT[u]
                                copy_q((13 if s < PAIRS - 2 or behind else 11) + g * ROUNDS - half,
                                       TB if half else S1[0], QTm[1 - s % 2], half, (0,))

                def router_exps(b):
                    act.wait_ge(s_soft, b + 1)
                    act.activation(R["exps"][:], R["work"][:], ACT.Exp).then_inc(s_softed, 1)

                for m in range(HALF):
                    copy_x(0, m)
                copy_q(2, S1[1], QT[0], 0)
                copy_q(3, TB, QT[0], 1)
                copy_q(4, S1[0], QTm[0], 0, (0,))
                copy_q(5, S1[1], QTm[0], 1, (0,))
                copy_q(6, TB, QT[1], 0)
                copy_q(7, TB, QT[1], 1)
                sequences(act, sequence)
                copy_o(G - 1)
                for m in range(HALF):
                    copy_to_all(B - 1, m, s_aturn, s_acopy)
                for m in range(HALF):
                    copy_to_all(B - 1, m, s_hturn, s_hcopy)
                router_exps(B - 1)

            @block.vector
            def _(dve):
                setup = Chain(dve, s_setup, 0)
                link = setup.link
                for t_ in (Qa[0], Qa[1], Ka):
                    link(dve.memset(t_[:, :, :, PRODUCTS:ROWS].bitcast(F32), 0.0))
                link(dve.memset(Ka[:, :, :, PRODUCTS:SCORED].bitcast(F32), 1.0))
                link(dve.memset(maxima[:], LOWEST))
                link(dve.memset(running[:], 0.0))
                link(dve.memset(same_expert[:], 1.0))
                link(dve.memset(same_expert[:, :, 0:1], 0.0))
                dve.wait_ge(s_const, 15)
                link(dve.tensor_scalar(zero_row[:, D:D + 1].bitcast(I32), token[:, 0:1], float(T), None, ALU.add))
                dve.sem_inc(s_dconst, 1)
                link(dve.tensor_scalar(e_start[:], e_index[:, :, 0], float(REGION), None, ALU.mult))
                dve.sem_inc(s_s1r, 3)
                dve.sem_inc(s_norm, 1)

                def rsqrt_step(chain, n, i):
                    var, rstd, newton = n["var"], n["rstd"], n["newton"]
                    if i == 0:
                        chain.step(lambda: dve.tensor_single_scalar(newton[:].bitcast(I32), var[:].bitcast(I32), 1,
                                                                    op=ALU.arith_shift_right))
                    elif i == 1:
                        chain.step(lambda: dve.tensor_scalar(rstd[:].bitcast(I32), newton[:].bitcast(I32), -1.0,
                                                             float(RSQRT_MAGIC), ALU.mult, ALU.add))
                    elif i % 3 == 2:
                        chain.step(lambda: dve.tensor_tensor(newton[:], rstd[:], rstd[:], ALU.mult))
                    elif i % 3 == 0:
                        chain.step(lambda: dve.scalar_tensor_tensor(out=newton[:], in0=newton[:], scalar=-0.5,
                                                                    in1=var[:], op0=ALU.mult, op1=ALU.mult))
                    else:
                        chain.step(lambda: dve.scalar_tensor_tensor(out=rstd[:], in0=newton[:], scalar=1.5,
                                                                    in1=rstd[:], op0=ALU.add, op1=ALU.mult))
                    if i == RSQRT_LINKS - 1:
                        chain.settle()

                def together(chain, instructions):
                    for last in instructions:
                        last.then_inc(chain.sem, 1)
                        chain.n += 1
                    dve.wait_ge(chain.sem, chain.base + chain.n)
                    dve.sem_inc(s_dve_passed, 1)

                def moments(chain, n, tiles):
                    together(chain, (dve.bn_aggr(n["moments"][:, t], n["stats"][:, t]) for t in range(tiles)))

                norm1_chain = Chain(dve, s_link1, 2 * (HALF + HALF + 1 + 11))

                def first_norm_step(b, half, i, src=xin):
                    chain = norm1_chain
                    if i < HALF:
                        if i == 0 and half == 0:
                            chain.begin(b)
                        if i == 0 and src is xin:
                            dve.wait_ge(s_x, 16 if isinstance(b, int) and b == 0 else (2 * b + half) * 16)
                        elif i == 0:
                            dve.wait_ge(s_res, 16)
                        dve.bn_stats(norm1["stats"][:, i], src[:, i]).then_inc(chain.sem, 1)
                        chain.n += 1
                    elif i == HALF:
                        chain.settle()
                        dve.sem_inc(s_dve_passed, 1)
                        moments(chain, norm1, HALF)
                        chain.link(dve.tensor_scalar(norm1["var"][:], norm1["moments"][:, :, 1], 1e-5, None, ALU.add))
                    else:
                        rsqrt_step(chain, norm1, i - HALF - 1)
                    if half == 1 and i == FIRST_STEPS - 1:
                        chain.end()

                def normalise_x(b, t, src=xin):
                    i = t % HALF
                    if t >= 2:
                        dve.wait_ge(s_xturn, b * HALF + t // 2)
                    dve.tensor_scalar(xn[:, t % 2], src[:, i], norm1["moments"][:, i, 0:1],
                                      norm1["rstd"][:, i:i + 1], ALU.subtract, ALU.mult).then_inc(s_xn, 1)

                def add_bias(b, t, i, bank):
                    dst = qkv_all[:, ds(b % 2 * NT + t, 1), :].rearrange("p a n -> p (a n)")
                    lo, hi = QKV_HALVES[i]
                    dve.wait_ge(s_qkvp, (b * NT + t) * 2 + i + 1)
                    dve.tensor_tensor(dst[:, lo:hi], bank[:, 0:hi - lo], qkv_bias[:, lo:hi], ALU.add)\
                        .then_inc(s_s1r, 1)

                def spare(position, uses):
                    dve.wait_ge(s_s1r, 3 + position)
                    dve.sem_inc(s_s1r, uses)

                def reduce_piece(g, c, bank):
                    j, qt, piece = PIECES[c]
                    n = min((qt + 1) * P - piece * 512, 512)
                    dve.wait_ge(s_s1, g * CHUNKS + c + 1)
                    dve.tensor_reduce(maxima[:, j, qt, piece:piece + 1], bank[:, 0:n], AX.X,
                                      ALU.max).then_inc(s_s1r, 1)

                def maxima_to_rows(g, par, position, half):
                    tiles, before = slice(half * HALF, (half + 1) * HALF), g * 4 + (1 - half) * 2
                    dve.wait_ge(s_s1r, 3 + position)
                    dve.tensor_reduce(top_score[:, :, tiles], maxima[:, :, tiles], AX.X, ALU.max).then_inc(s_mstep, 1)
                    dve.wait_ge(s_mstep, before + 1)
                    top = top_score[:, :, tiles].rearrange("p j t -> p t j")
                    hi = Qa[par][:, tiles, :, PRODUCTS]
                    dve.tensor_scalar(hi, top, -1.0, None, ALU.mult).then_inc(s_mstep, 1)
                    dve.wait_ge(s_mstep, before + 2)
                    dve.scalar_tensor_tensor(out=Qa[par][:, tiles, :, PRODUCTS + 1], in0=top, scalar=-1.0,
                                             in1=hi.bitcast(F32), op0=ALU.mult,
                                             op1=ALU.subtract).then_inc(s_m, 1)

                def copy_k(n, bank, par, half):
                    dve.wait_ge(s_round, n + 1)
                    dve.tensor_copy(KT[par][:, half * 512:(half + 1) * 512], bank[:]).then_inc(s_k, 1)

                def copy_q_max(n, par, half, bank):
                    dve.wait_ge(s_round, n + 1)
                    dve.tensor_copy(QTm[par][1][ROWS:P, half * 512:(half + 1) * 512], bank[ROWS:P, :])\
                        .then_inc(s_qm, 1)

                def normalise(g, s):
                    dve.wait_ge(s_ot, g + 1)
                    turned = TB[:, :].rearrange("p (u g r) -> p u g r", u=HALF, g=4)
                    dve.reciprocal(rden[:], turned[:, :, :, HD]).then_inc(s_nstep, 1)
                    dve.wait_ge(s_nstep, g + 1)
                    for h in range(2):
                        dst = attn[:, h * HALF:(h + 1) * HALF, s * 2 * HD:(s + 1) * 2 * HD]
                        last = dve.tensor_tensor(
                            dst.rearrange("p u (j d) -> p u j d", j=2),
                            turned[:, :, 2 * h:2 * h + 2, 0:HD],
                            rden[:, :, 2 * h:2 * h + 2].unsqueeze(3).to_broadcast([P, HALF, 2, HD]), ALU.mult)
                    last.then_inc(s_norm, 1)

                norm2_chain = Chain(dve, s_link2, ROUTE_LINKS)
                link2 = norm2_chain.link

                def over_e(v):
                    return v[:].unsqueeze(1).to_broadcast([P, E, NT])

                def by_token(r):
                    return r[:].rearrange("p e t -> p t e")

                def residual(b, t, bank):
                    if t == 0:
                        norm2_chain.begin(b)
                        dve.wait_ge(s_resb, b + 1)
                    dve.wait_ge(s_proj, b * NT + t + 1)
                    dve.tensor_tensor(xres[:, t], bank[:, 0:D], xres[:, t], ALU.add).then_inc(s_x2, 1)
                    dve.wait_ge(s_x2, b * NT + t + 1)
                    dve.bn_stats(norm2["stats"][:, t], xres[:, t]).then_inc(s_link2, 1)
                    norm2_chain.n += 1

                def second_norm_step(i):
                    if i == 0:
                        dve.wait_ge(s_link2, norm2_chain.base + norm2_chain.n)
                        dve.sem_inc(s_dve_passed, 1)
                        moments(norm2_chain, norm2, NT)
                    elif i == 1:
                        link2(dve.tensor_scalar(norm2["var"][:], norm2["moments"][:, :, 1], 1e-5, None, ALU.add))
                    else:
                        rsqrt_step(norm2_chain, norm2, i - 2)

                def normalise_rows(t):
                    dve.tensor_scalar(rows[0][:, t, 0:D], xres[:, t], norm2["moments"][:, t, 0:1],
                                      norm2["rstd"][:, t:t + 1], ALU.subtract, ALU.mult).then_inc(s_h, 1)

                def rms_step(i):
                    if i == 0:
                        link2(dve.tensor_tensor(rnorm["newton"][:], norm2["rstd"][:], norm2["rstd"][:], ALU.mult))
                        link2(dve.tensor_tensor(rnorm["newton"][:], rnorm["newton"][:], norm2["moments"][:, :, 1],
                                                ALU.mult))
                    elif i == 1:
                        link2(dve.tensor_scalar(rnorm["var"][:], rnorm["newton"][:], 1e-6, None, ALU.add))
                    else:
                        rsqrt_step(norm2_chain, rnorm, i - 2)
                    if i == NORM_STEPS - 1:
                        link2(dve.tensor_scalar(V1["w"][:], rnorm["rstd"][:], float(D) ** -0.5, None, ALU.mult))

                def logits(b, bank):
                    dve.wait_ge(s_logit, b + 1)
                    link2(dve.tensor_tensor(R["logits"][:], bank[:, 0:NT * E].rearrange("p (t e) -> p e t", e=E),
                                            over_e(V1["w"]), ALU.mult))
                    dve.sem_inc(s_s1r, 3)

                def pick(k):
                    left, work, chosen = R["logits" if k == 0 else "left"], R["work"], R[f"pick{k}"]
                    if k == 1:
                        link2(dve.tensor_reduce(V1["best"][:], by_token(left), AX.X, ALU.max))
                    link2(dve.tensor_tensor(work[:], left[:], over_e(V1["best"]), ALU.is_equal))
                    link2(dve.scalar_tensor_tensor(out=work[:], in0=work[:], scalar=-float(E), in1=e_index[:],
                                                   op0=ALU.mult, op1=ALU.add))
                    link2(dve.tensor_reduce(V1["index"][:], by_token(work), AX.X, ALU.min))
                    link2(dve.tensor_tensor(chosen[:], work[:], over_e(V1["index"]), ALU.is_equal))
                    if k == 0:
                        link2(dve.scalar_tensor_tensor(out=R["left"][:], in0=chosen[:], scalar=LOWEST,
                                                       in1=left[:], op0=ALU.mult, op1=ALU.add))

                def shift_logits():
                    link2(dve.tensor_reduce(V1["best"][:], by_token(R["logits"]), AX.X, ALU.max))
                    link2(dve.tensor_tensor(R["work"][:], R["logits"][:], over_e(V1["best"]), ALU.subtract))
                    dve.sem_inc(s_soft, 1)

                def count():
                    link2(dve.tensor_tensor(R["chosen"][:], R["pick0"][:], R["pick1"][:], ALU.add))
                    link2(dve.tensor_tensor_scan(R["count"][:].rearrange("p e t -> p (e t)"),
                                                 same_expert[:].rearrange("p e t -> p (e t)"),
                                                 R["chosen"][:].rearrange("p e t -> p (e t)"), 0.0,
                                                 ALU.mult, ALU.add))
                    dve.sem_inc(s_chosen, 1)

                def softmax():
                    exps, work = R["exps"], R["work"]
                    link2(dve.tensor_reduce(V1["sum"][:], by_token(exps), AX.X, ALU.add))
                    link2(dve.reciprocal(V1["rsum"][:], V1["sum"][:]))
                    link2(dve.tensor_tensor(exps[:], exps[:], over_e(V1["rsum"]), ALU.mult))
                    link2(dve.tensor_tensor(work[:], exps[:], R["chosen"][:], ALU.mult))
                    link2(dve.tensor_reduce(V1["gate"][:], by_token(work), AX.X, ALU.add))

                def weights():
                    exps = R["exps"]
                    link2(dve.tensor_scalar(V1["flag"][:], V1["gate"][:], 0.0, None, ALU.is_le))
                    link2(dve.tensor_tensor(V1["gate"][:], V1["gate"][:], V1["flag"][:], ALU.add))
                    link2(dve.reciprocal(V1["rsum"][:], V1["gate"][:]))
                    link2(dve.tensor_tensor(exps[:], exps[:], over_e(V1["rsum"]), ALU.mult))
                    link2(dve.tensor_tensor(exps[:], exps[:], escale[:].unsqueeze(2).to_broadcast([P, E, NT]),
                                            ALU.mult))

                def ranks(b, bank):
                    dve.wait_ge(s_rank, b + 1)
                    link2(dve.tensor_tensor(tail_f[:], running[:], e_start[:], ALU.add))
                    link2(dve.tensor_tensor(R["slot"][:], bank[:, 0:E * NT].rearrange("p (e t) -> p e t", t=NT),
                                            tail_f[:].unsqueeze(2).to_broadcast([P, E, NT]), ALU.add))
                    link2(dve.tensor_tensor(running[:], bank[:, E * NT:E * NT + E], running[:], ALU.add))
                    dve.sem_inc(s_s1r, 3)

                def place(b, k):
                    work = R["work"]
                    link2(dve.tensor_tensor(work[:], R[f"pick{k}"][:], R["exps"][:], ALU.mult))
                    link2(dve.tensor_reduce(rows[k][:, :, D + 1], by_token(work), AX.X, ALU.add))
                    link2(dve.tensor_copy(rows[k][:, :, D].bitcast(I32), token[:]))
                    link2(dve.tensor_tensor(work[:], R[f"pick{k}"][:], R["slot"][:], ALU.mult))
                    link2(dve.tensor_reduce(V1["dest"][:], by_token(work), AX.X, ALU.add))
                    dve.tensor_copy(slot_index[k][:], V1["dest"][:]).then_inc(s_slot, 1)
                    dve.wait_ge(s_slot, b * TOP + k + 1)
                    if k == TOP - 1:
                        link2(dve.tensor_scalar(token[:], token[:], float(S), None, ALU.add))
                        norm2_chain.end()

                def beside(b, s, u, before, behind, position):
                    if behind:
                        if s == 0:
                            first_norm_step(b + 1, 0, u)
                        if 1 <= s <= 4 and u < 2:
                            normalise_x(b + 1, 2 * (s - 1) + u)
                        if s == 2 and u >= 3:
                            for i in {3: (0, 1), 4: (2, 3), UNITS - 1: (UNITS - 2, UNITS - 1)}.get(u, (u - 1,)):
                                first_norm_step(b + 1, 1, i)
                    if projected_at(s, u):
                        t, i = projected_at(s, u)
                        if i < 2 and behind:
                            add_bias(b + 1, t, i, beside_bank(s, u))
                        elif i == 2 and before:
                            residual(b - 1, t, beside_bank(s, u))
                            dve.sem_inc(s_s1r, 1)
                        else:
                            spare(position, 1)
                    if before:
                        if s == 4 and u > 12:
                            second_norm_step(u - 13)
                        if s == 5 and u < 5:
                            second_norm_step(3 + 2 * u)
                            second_norm_step(4 + 2 * u)
                        if s == 5 and 5 <= u < 5 + NT:
                            if u == 5:
                                dve.wait_ge(s_listed, b)
                            normalise_rows(u - 5)
                        if s == 6 and u < 12:
                            rms_step(u)
                            if u == 11:
                                rms_step(12)
                        if (s, u) == ROUTER_AT:
                            logits(b - 1, beside_bank(s, u))
                        if (s, u) == (6, 12):
                            shift_logits()
                        if (s, u) in ((6, 15), (7, 0)):
                            if s == 6:
                                dve.wait_ge(s_softed, b)
                            pick(s - 6)
                        if (s, u) == (7, 1):
                            count()
                        if (s, u) == (7, 7):
                            softmax()
                        if (s, u) == (7, 8):
                            weights()
                        if (s, u) == RANK_AT:
                            ranks(b - 1, beside_bank(s, u))
                        if (s, u) in ((7, 12), (7, 13)):
                            place(b - 1, u - 12)
                    elif (s, u) in (ROUTER_AT, RANK_AT):
                        spare(position, 3)

                def sequence(b, before, behind):
                    for s in range(PAIRS):
                        g, par = b * PAIRS + s, s % 2
                        more = s < PAIRS - 1 or behind
                        c = 0
                        for u in range(UNITS):
                            while more and c < pieces_after(u):
                                reduce_piece(g + 1, c, S1[(beside_before(s, u) + c) % 3])
                                c += 1
                            if u == 1 and (s or before):
                                normalise(g - 1, (s - 1) % PAIRS)
                            if u in MAX_AT and more:
                                half = MAX_AT[u]
                                pieces = LATER_PIECES if half else CHUNKS
                                maxima_to_rows(g + 1, 1 - par, s1_position(b, s) + beside_before(s, u) + pieces, half)
                                if s == NT // 2 and behind and half == 0:
                                    dve.sem_inc(s_qkv, 1)
                            beside(b, s, u, before, behind, s1_position(b, s) + beside_before(s, u) + c)
                            if u in MAX_TURN_AT and more:
                                half = MAX_TURN_AT[u]
                                copy_q_max((13 if s < PAIRS - 2 or behind else 11) + g * ROUNDS - half, 1 - par,
                                           half, TB if half else S1[0])
                        if s < PAIRS - 2 or behind:
                            copy_k(14 + g * ROUNDS, S1[1], par, 0)
                            copy_k(15 + g * ROUNDS, S1[2], par, 1)

                def first_tiles(t, src):
                    for i in range(2):
                        normalise_x(0, t + i, src)

                def first_bias(t):
                    for n in range(2 * t, 2 * t + 4):
                        add_bias(0, n // 2, n % 2, S1[n % 3])

                for i in range(FIRST_STEPS):
                    first_norm_step(0, 0, i)
                for t in range(0, HALF, 2):
                    first_tiles(t, xin)
                later = xres[:, HALF:NT]
                for i in range(FIRST_STEPS):
                    first_norm_step(0, 1, i, later)
                for t in range(HALF, NT, 2):
                    first_bias(t - HALF)
                    first_tiles(t, later)
                for i in range(2):
                    for turned_q in (QT[i], QTm[i]):
                        link(dve.memset(turned_q[0][ROWS:P].bitcast(F32), 0.0))
                        link(dve.memset(turned_q[1][0:ROWS].bitcast(F32), 0.0))
                dve.wait_ge(s_wq, 16 * 7)
                for c in range(DC):
                    link(dve.tensor_scalar(router[:, c], router_raw[:, c], scale_raw[:, c:c + 1], None, ALU.mult))
                for t in range(HALF, NT, 2):
                    first_bias(t)
                spare(2 * NT, 2)
                dve.sem_inc(s_qkv, 1)
                copy_k(0, TB, 0, 0)
                copy_k(1, S1[0], 0, 1)
                for c in range(CHUNKS):
                    reduce_piece(0, c, S1[c % 3])
                for half in (1, 0):
                    maxima_to_rows(0, 0, STARTUP, half)
                for half in range(2):
                    copy_q_max(4 + half, 0, half, S1[half])
                copy_k(8, TB, 1, 0)
                copy_k(9, S1[2], 1, 1)
                sequences(dve, sequence)
                normalise(G - 1, PAIRS - 1)

                for t in range(NT):
                    residual(B - 1, t, S1[t % 3])
                for i in range(NORM_STEPS):
                    second_norm_step(i)
                dve.wait_ge(s_listed, B)
                for t in range(NT):
                    normalise_rows(t)
                for i in range(NORM_STEPS):
                    rms_step(i)
                logits(B - 1, S1[0])
                shift_logits()
                dve.wait_ge(s_softed, B)
                for k in range(TOP):
                    pick(k)
                count()
                softmax()
                weights()
                ranks(B - 1, S1[0])
                for k in range(TOP):
                    place(B - 1, k)
                end = Chain(dve, s_end, 0)
                link = end.link
                link(dve.tensor_tensor(tail_f[:], running[:], e_start[:], ALU.add))
                link(dve.tensor_scalar(tail_index[:], tail_f[:], token[:, 0:1], -float(T), ALU.add, ALU.add))
                dve.sem_inc(s_tail, 1)
                most = T // P
                big = work[0:1].rearrange("p a n -> p (a n)")
                sizes = big[:, 0:E * most].rearrange("p (e j) -> p e j", e=E)
                reached_end = big[:, E * most + MT * E:]
                reached = big[:, E * most:E * most + MT * E].rearrange("p (s e) -> p s e", e=E)
                weighed = reached_end[:, 0:MT * E].rearrange("p (s e) -> p s e", e=E)
                small = xin[0:1].rearrange("p t d -> p (t d)")
                tiles, ends = small[:, 0:E], small[:, E:2 * E]
                count, which, first, local = (small[:, 64 + n * MT:64 + (n + 1) * MT] for n in range(4))
                link(dve.tensor_tensor(sizes, running[0:1].unsqueeze(2).to_broadcast([1, E, most]),
                                       tile_start[:].unsqueeze(1).to_broadcast([1, E, most]), ALU.is_gt))
                link(dve.tensor_reduce(tiles, sizes, AX.X, ALU.add))
                link(dve.tensor_tensor_scan(ends, ones[0:1, 0:E], tiles, 0.0, ALU.mult, ALU.add))
                link(dve.tensor_tensor(reached, step_index[:].unsqueeze(2).to_broadcast([1, MT, E]),
                                       ends.unsqueeze(1).to_broadcast([1, MT, E]), ALU.is_ge))
                link(dve.tensor_reduce(which, reached, AX.X, ALU.add))
                link(dve.tensor_tensor(weighed, reached, tiles.unsqueeze(1).to_broadcast([1, MT, E]), ALU.mult))
                link(dve.tensor_reduce(first, weighed, AX.X, ALU.add))
                link(dve.tensor_tensor(local, step_index[:], first, ALU.subtract))
                link(dve.tensor_scalar(count, which, float(E), float(P), ALU.is_lt, ALU.mult))
                link(dve.tensor_tensor(local, local, count, ALU.mult))
                link(dve.scalar_tensor_tensor(out=table_row[:], in0=which, scalar=float(REGION), in1=local,
                                              op0=ALU.mult, op1=ALU.add))
                link(dve.tensor_scalar(table_expert[:], which, float(E - 1), None, ALU.min))

            @block.tensor
            def _(pe):
                pe.sem_inc(s_pv, 2)
                pe.wait_ge(s_const, 15)
                pe.wait_ge(s_dconst, 1)

                def turn(tiles, ready, free, n):
                    pe.wait_ge(free, n + 1)
                    for c in range(DC):
                        for r in range(2):
                            last = pe.transpose(TB[:, (2 * c + r) * P:(2 * c + r + 1) * P],
                                                tiles(r)[:, c * P:(c + 1) * P], ident[:])
                    last.then_inc(ready, 1)

                def turn_x(b, m):
                    pe.wait_ge(s_xn, b * NT + 2 * m + 2)
                    turn(lambda r: xn[:, r], s_xturn, s_xcopy, b * HALF + m)

                def turn_attn(b, m):
                    turn(lambda r: attn[:, 2 * m + r], s_aturn, s_acopy, b * HALF + m)

                def turn_h(b, m):
                    turn(lambda r: rows[0][:, 2 * m + r, 0:D], s_hturn, s_hcopy, b * HALF + m)

                def project(b, t, i, position, bank):
                    lo, hi = QKV_HALVES[i]
                    pe.wait_ge(s_xcopy, 1 + b * HALF + t // 2 + 1)
                    pe.wait_ge(s_s1r, position + 1)
                    for c in range(DC):
                        last = pe.matmul(bank[:, 0:hi - lo], xT[:, c, t % 2], wqkv[:, c, lo:hi],
                                         start=(c == 0), stop=(c == DC - 1))
                    last.then_inc(s_qkvp, 1)

                def project_out(b, t, bank):
                    pe.wait_ge(s_acopy, 1 + (b + 1) * HALF)
                    for c in range(DC):
                        last = pe.matmul(bank[:, 0:D], turned_all[:, c, t * P:(t + 1) * P], wout[:, c],
                                         start=(c == 0), stop=(c == DC - 1))
                    last.then_inc(s_proj, 1)

                def router_logits(b, bank):
                    pe.wait_ge(s_hcopy, 1 + (b + 1) * HALF)
                    for t in range(NT):
                        for c in range(DC):
                            last = pe.matmul(bank[:, t * E:(t + 1) * E], turned_all[:, c, t * P:(t + 1) * P],
                                             router[:, c], start=(c == 0), stop=(c == DC - 1))
                    last.then_inc(s_logit, 1)

                def rank(b, bank):
                    pe.wait_ge(s_chosen, b + 1)
                    pe.matmul(bank[:, 0:E * NT], not_before[:], R["chosen"][:].rearrange("p e t -> p (e t)"),
                              start=True, stop=False)
                    pe.matmul(bank[:, 0:E * NT], ones[:], R["count"][:].rearrange("p e t -> p (e t)"),
                              start=False, stop=True)
                    pe.matmul(bank[:, E * NT:E * NT + E], ones[:], R["count"][:, :, NT - 1],
                              start=True, stop=True).then_inc(s_rank, 1)

                def round_(bank, src, half):
                    for i in range(HALF):
                        tile = src[:, half * HALF + i].rearrange("p j r -> p (j r)").bitcast(F32)
                        last = pe.transpose(bank[:, i * P:(i + 1) * P], tile, ident[:])
                    last.then_inc(s_round, 1)

                def scores(g, par, c, position, bank):
                    j, qt, piece = PIECES[c]
                    lo = piece * 512
                    n = min((qt + 1) * P - lo, 512)
                    diagonal = lo + n == (qt + 1) * P
                    pe.wait_ge(s_s1r, position + 1)
                    last = pe.matmul(bank[:, 0:n], QT[par][j][:, qt * P:(qt + 1) * P], KT[par][:, lo:lo + n],
                                     start=True, stop=not diagonal)
                    if diagonal:
                        last = pe.matmul(bank[:, n - P:n], identb[:], mask_qk[:], start=False, stop=True)
                    last.then_inc(s_s1, 1)

                def shifted(g, par, u, copied):
                    kt, j = u // 2, u % 2
                    for n, (v, lo, hi) in enumerate(PARTS):
                        if v != u:
                            continue
                        pe.wait_ge(s_e, g * NP + n + 1)
                        if u == 0 and lo == 0:
                            pe.wait_ge(s_q, copied)
                        if u == 1 and lo == 0:
                            pe.wait_ge(s_qm, 2 * (g + 1))
                        bank, at, end = S2[n % 3], lo % 512, (hi - 1) % 512 + 1
                        diagonal = lo == kt * P
                        last = pe.matmul(bank[:, at:end], KT[par][:, kt * P:(kt + 1) * P], QTm[par][j][:, lo:hi],
                                         start=True, stop=not diagonal)
                        if diagonal:
                            last = pe.matmul(bank[:, at:at + P], identb[:], mask_kq[:], start=False, stop=True)
                        last.then_inc(s_s2, 1)

                def values(g, par, kt, h):
                    pe.wait_ge(s_e, 3 + g * NP + parts_before(2 * kt + 2))
                    if kt == 0 and h == 0:
                        pe.wait_ge(s_o, g + 1)
                        pe.wait_ge(s_v, g + 1)
                    lo, hi = max(h * 512, kt * P), (h + 1) * 512
                    if lo >= hi:
                        return
                    for j in range(2):
                        q = 32 * (2 * h + j)
                        last = pe.matmul(OB[q:q + 32, lo - h * 512:512], V[par][:, kt, j],
                                         probs[:, (2 * kt + j) % 4, lo:hi], start=(kt == 0),
                                         stop=(kt == HALF * (h + 1) - 1))
                    if h == 1:
                        last.then_inc(s_pv, 1)

                def turn_output(g):
                    pe.wait_ge(s_o, 1 + g + 1)
                    for i in range(HALF):
                        last = pe.transpose(TB[:, i * P:(i + 1) * P], OT[:, i * P:(i + 1) * P], ident[:])
                    last.then_inc(s_ot, 1)

                def beside(b, s, u, before, behind, position):
                    g = b * PAIRS + s
                    if (s, u) == (0, 4) or (u == 3 and 1 <= s <= 4) or (s, u) == (6, 3):
                        pe.wait_ge(s_norm, 1 + g)
                    t = attn_turned_at(s, u)
                    if before and t is not None:
                        turn_attn(b - 1, t)
                    t = turned_at(s, u)
                    if behind and t is not None:
                        turn_x(b + 1, t)
                    t = h_turned_at(s, u)
                    if before and t is not None:
                        if t == 0:
                            pe.wait_ge(s_h, b * NT)
                        turn_h(b - 1, t)
                    if projected_at(s, u):
                        t, i = projected_at(s, u)
                        if i < 2 and behind:
                            project(b + 1, t, i, position, beside_bank(s, u))
                        if i == 2 and before:
                            pe.wait_ge(s_s1r, position + 1)
                            project_out(b - 1, t, beside_bank(s, u))
                    if before and (s, u) == ROUTER_AT:
                        pe.wait_ge(s_s1r, position + 1)
                        router_logits(b - 1, beside_bank(s, u))
                    if before and (s, u) == RANK_AT:
                        pe.wait_ge(s_s1r, position + 1)
                        rank(b - 1, beside_bank(s, u))

                def sequence(b, before, behind):
                    for s in range(PAIRS):
                        g, par = b * PAIRS + s, s % 2
                        more = s < PAIRS - 1 or behind
                        more2 = s < PAIRS - 2 or behind
                        position = s1_position(b, s)
                        c = 0
                        for u in range(UNITS):
                            shifted(g, par, u, 6 + 4 * g if more else 4 * G)
                            if u == 0 and (s or before):
                                values(g - 1, 1 - par, NT - 1, 1)
                            halves = [0, 1] if u % 2 and u >= 3 else []
                            while more and c < pieces_after(u):
                                if c == 0:
                                    pe.wait_ge(s_k, 4 + 2 * g)
                                uses = beside_before(s, u) + c
                                scores(g + 1, 1 - par, c, position + uses, S1[uses % 3])
                                c += 1
                                if halves:
                                    values(g, par, u // 2 - 1, halves.pop(0))
                            for h in halves:
                                values(g, par, u // 2 - 1, h)
                            if u == 1 and (s or before):
                                turn_output(g - 1)
                            beside(b, s, u, before, behind, position + beside_before(s, u) + c)
                            if u in Q_AT and more2:
                                half = Q_AT.index(u)
                                if half == 0:
                                    pe.wait_ge(s_build, g + 3)
                                    pe.wait_ge(s_norm, 1 + g)
                                    if behind and turned_at(s, 3) is not None:
                                        pe.wait_ge(s_xcopy, 1 + (b + 1) * HALF + turned_at(s, 3) + 1)
                                    if before and s == 0:
                                        pe.wait_ge(s_acopy, 1 + b * HALF)
                                    if before and s == 6:
                                        pe.wait_ge(s_hcopy, 1 + b * HALF)
                                else:
                                    pe.wait_ge(s_q, 6 + 4 * g + 1)
                                round_(TB, Qa[par], half)
                            if u in MAX_TURN_AT and more:
                                half = MAX_TURN_AT[u]
                                pe.wait_ge(s_m, 2 * (g + 1) + 2 - half)
                                if half == 0:
                                    pe.wait_ge(s_s1r, 3 + position + beside_before(s, u) + CHUNKS)
                                elif more2:
                                    pe.wait_ge(s_q, 6 + 4 * g + 2)
                                else:
                                    pe.wait_ge(s_norm, 1 + g)
                                    pe.wait_ge(s_hcopy, 1 + b * HALF)
                                round_(TB if half else S1[0], Qa[1 - par], half)
                        if more2:
                            round_(S1[1], Ka, 0)
                            round_(S1[2], Ka, 1)

                pe.wait_ge(s_wq, 16 * 7)
                for m in range(HALF):
                    turn_x(0, m)
                    for n in range(4 * m, 4 * m + 4):
                        project(0, n // 2, n % 2, n, S1[n % 3])
                pe.wait_ge(s_s1r, 3 + FIRST_USES)
                pe.wait_ge(s_build, 1)
                round_(TB, Ka, 0)
                round_(S1[0], Ka, 1)
                round_(S1[1], Qa[0], 0)
                pe.wait_ge(s_k, 1)
                round_(TB, Qa[0], 1)
                pe.wait_ge(s_q, 2)
                pe.wait_ge(s_k, 2)
                for c in range(CHUNKS):
                    scores(0, 0, c, FIRST_USES + c, S1[c % 3])
                pe.wait_ge(s_m, 2)
                for half in range(2):
                    round_(S1[half], Qa[0], half)
                pe.wait_ge(s_build, 2)
                round_(TB, Qa[1], 0)
                pe.wait_ge(s_q, 5)
                round_(TB, Qa[1], 1)
                pe.wait_ge(s_q, 6)
                round_(TB, Ka, 0)
                round_(S1[2], Ka, 1)
                sequences(pe, sequence)
                values(G - 1, 1, NT - 1, 1)
                turn_output(G - 1)

                pe.wait_ge(s_norm, 1 + G)
                for m in range(HALF):
                    turn_attn(B - 1, m)
                for t in range(NT):
                    if t >= 3:
                        pe.wait_ge(s_x2, (B - 1) * NT + t - 2)
                    project_out(B - 1, t, S1[t % 3])
                pe.wait_ge(s_h, B * NT)
                for m in range(HALF):
                    turn_h(B - 1, m)
                router_logits(B - 1, S1[0])
                rank(B - 1, S1[0])

        xe = rows[0]
        ye = rows[1]
        gelu_, acts, actT = (work[:, i].rearrange("p (r n) -> p r n", r=2) for i in range(3))
        gate_banks = ((S2[0], S2[1]), (S2[2], S1[2]))
        RING = 4
        assert MT % RING == 0
        
        q_xe = [sem(f"expert_rows_in{r}") for r in range(RING)]
        q_out = sem("results_added")
        q_xt = sem("expert_x_turned"); q_xtc = sem("expert_x_copied"); q_g = sem("gates_summed")
        q_gelu = sem("gelu_ready"); q_act = sem("act_ready"); q_at = sem("act_turned"); q_atc = sem("act_copied")
        q_dn = sem("down_summed"); q_y = sem("y_ready")

        with nc.Block() as block:

            @block.sync
            def _(sp):

                def load_rows(q, r):
                    row = sp.value_load(table_row[0:1, ds(q * RING + r, 1)], min_val=0, max_val=ZEROS)
                    if not isinstance(q, int):
                        sp.wait_ge(q_out, 16 * (q * RING + r - RING + 1))
                    sp.dma_start(xe[:, r, :], routed[ds(row, P), :]).then_inc(q_xe[r], 16)

                for r in range(RING):
                    load_rows(0, r)
                with sp.Fori(1, MT // RING, 1) as q:
                    for r in range(RING):
                        load_rows(q, r)

            @block.gpsimd
            def _(pool):
                def add_results(i, r):
                    pool.wait_ge(q_y, 2 + i + 1)
                    if r or not isinstance(i, int):
                        pool.wait_ge(q_out, 16 * i)
                    pool.sem_inc(s_pool_passed, 1)
                    pool.indirect_dma_start(
                        sums[:, :], bass.IndirectOffsetOnAxis(ap=xe[:, r, D:D + 1].bitcast(I32), axis=0),
                        ye[:, r, 0:D], None, compute_op=ALU.add).then_inc(q_out, 16)

                for r in range(RING):
                    add_results(r, r)
                with pool.Fori(1, MT // RING, 1) as q:
                    for r in range(RING):
                        add_results(q * RING + r, r)
                pool.wait_ge(q_out, 16 * MT)

            @block.scalar
            def _(act):
                act.sem_inc(q_xtc, 1)
                act.sem_inc(q_atc, 1)

                def copy_x(i, r):
                    act.wait_ge(q_xt, i + 1)
                    act.activation(xT[:, :, r % 2], TB[:, 0:D].rearrange("p (c m) -> p c m", c=DC),
                                   ACT.Copy).then_inc(q_xtc, 1)

                def gelu(i, r):
                    act.wait_ge(q_g, 2 * i + 1)
                    act.wait_ge(q_act, i + 1)
                    act.activation(gelu_[:, r % 2], gate_banks[r % 2][0][:, 0:HID], ACT.Gelu_apprx_tanh).then_inc(q_gelu, 1)

                def copy_act(i, r):
                    act.wait_ge(q_at, 2 + i + 1)
                    act.activation(actT[:, r % 2], OB[:, 0:HID], ACT.Copy).then_inc(q_atc, 1)

                def group(base, last):
                    for r in range(RING):
                        i = base + r
                        copy_act(i, r)
                        if not (last and r == RING - 1):
                            gelu(i + 1, r + 1)
                        if not (last and r >= RING - 2):
                            copy_x(i + 2, r)

                copy_x(0, 0)
                gelu(0, 0)
                copy_x(1, 1)
                with act.Fori(0, MT // RING - 1, 1) as q:
                    group(q * RING, False)
                group(MT - RING, True)

            @block.vector
            def _(dve):
                dve.sem_inc(q_act, 2)
                dve.sem_inc(q_y, 2)

                def multiply(i, r):
                    dve.wait_ge(q_gelu, i + 1)
                    dve.wait_ge(q_g, 2 * i + 2)
                    dve.wait_ge(q_at, i + 1)
                    dve.tensor_tensor(acts[:, r % 2], gelu_[:, r % 2], gate_banks[r % 2][1][:, 0:HID],
                                      ALU.mult).then_inc(q_act, 1)

                def weigh(i, q, r):
                    dve.wait_ge(q_dn, i + 1)
                    if q is not None:
                        dve.wait_ge(q_out, 16 * (i - RING + 1))
                    dve.tensor_scalar(ye[:, r, 0:D], S1[r % 2][:, 0:D], xe[:, r, D + 1:D + 2], None,
                                      ALU.mult).then_inc(q_y, 1)

                def group(q, base, last):
                    for r in range(RING):
                        if not (last and r == RING - 1):
                            multiply(base + r + 1, r + 1)
                        weigh(base + r, q, r)

                multiply(0, 0)
                group(None, 0, False)
                with dve.Fori(1, MT // RING - 1, 1) as q:
                    group(q, q * RING, False)
                group(MT // RING - 1, MT - RING, True)

            @block.tensor
            def _(pe):
                pe.sem_inc(q_at, 2)

                def expert(i):
                    return pe.value_load(table_expert[0:1, ds(i, 1)], min_val=0, max_val=E - 1)

                def turn_x(i, q, r):
                    pe.wait_ge(q_xe[r], 16 * (q + 1))
                    pe.wait_ge(q_xtc, i + 1)
                    for c in range(DC):
                        last = pe.transpose(TB[:, c * P:(c + 1) * P], xe[:, r, c * P:(c + 1) * P], ident[:])
                    last.then_inc(q_xt, 1)

                def gates(i, r, n):
                    e = expert(i)
                    pe.wait_ge(q_xtc, 1 + i + 1)
                    pe.wait_ge(q_act, i + 1)
                    for c in range(DC):
                        w = wg[c][:, ds(e, 1), n * HID:(n + 1) * HID].rearrange("p a h -> p (a h)")
                        last = pe.matmul(gate_banks[r % 2][n][:, 0:HID], xT[:, c, r % 2], w,
                                         start=(c == 0), stop=(c == DC - 1))
                    last.then_inc(q_g, 1)

                def turn_act(i, r):
                    pe.wait_ge(q_act, 2 + i + 1)
                    pe.wait_ge(q_atc, i + 1)
                    for c in range(HC):
                        last = pe.transpose(OB[:, c * P:(c + 1) * P], acts[:, r % 2, c * P:(c + 1) * P], ident[:])
                    last.then_inc(q_at, 1)

                def down(i, r):
                    e = expert(i)
                    pe.wait_ge(q_atc, 1 + i + 1)
                    pe.wait_ge(q_y, i + 1)
                    for c in range(HC):
                        w = wl[:, c, ds(e, 1), :].rearrange("p a d -> p (a d)")
                        last = pe.matmul(S1[r % 2][:, 0:D], actT[:, r % 2, c * P:(c + 1) * P], w,
                                         start=(c == 0), stop=(c == HC - 1))
                    last.then_inc(q_dn, 1)

                def group(q, base, last):
                    for r in range(RING):
                        i = base + r
                        if not (last and r == RING - 1):
                            gates(i + 1, r + 1, 0)
                        turn_act(i, r)
                        if not (last and r == RING - 1):
                            gates(i + 1, r + 1, 1)
                        if not (last and r >= RING - 2):
                            turn_x(i + 2, q + (r + 2) // RING, (r + 2) % RING)
                        down(i, r)

                turn_x(0, 0, 0)
                pe.wait_ge(s_wg, 16 * WEIGHT_LOADS)
                gates(0, 0, 0)
                gates(0, 0, 1)
                turn_x(1, 0, 1)
                with pe.Fori(0, MT // RING - 1, 1) as q:
                    group(q, q * RING, False)
                group(MT // RING - 1, MT - RING, True)

        f_out = [sem(f"result_out{n}") for n in range(2)]
        halves = [(v[n * (T // 2):(n + 1) * (T // 2)].rearrange("(p r) d -> p (r d)", p=P))
                  for n in range(2) for v in (out.rearrange("b s d -> (b s) d"), sums)]

        with nc.Block() as block:

            @block.sync
            def _(sp):
                sp.dma_start(halves[0], halves[1]).then_inc(f_out[0], 16)
                sp.wait_ge(f_out[0], 16)

            @block.scalar
            def _(act):
                act.dma_start(halves[2], halves[3]).then_inc(f_out[1], 16)
                act.wait_ge(f_out[1], 16)


def kernel(L0_attn_x, L0_attn_qkv_w, L0_attn_qkv_b, L0_attn_out_w, L0_attn_out_b, L0_ffn_router_scale,
           L0_ffn_router_w, L0_ffn_gating_w, L0_ffn_linear_w, L0_ffn_per_expert_scale):
    import numpy as np
    import concourse.bacc as bacc
    from concourse.bass_utils import run_bass_kernel_spmd

    nc = bacc.Bacc("TRN2", target_bir_lowering=False, num_devices=1)
    given = {"x": L0_attn_x, "qkv_w": L0_attn_qkv_w, "qkv_b": L0_attn_qkv_b, "out_w": L0_attn_out_w,
             "out_b": L0_attn_out_b, "router_scale": L0_ffn_router_scale, "router_w": L0_ffn_router_w,
             "gate_w": np.transpose(np.asarray(L0_ffn_gating_w), (3, 0, 1, 2)), "linear_w": L0_ffn_linear_w,
             "expert_scale": L0_ffn_per_expert_scale}
    arrays, args = {}, []
    for name, value in given.items():
        a = np.ascontiguousarray(value)
        arrays[name] = a
        args.append(nc.dram_tensor(name, a.shape, mybir.dt.from_np(a.dtype), kind="ExternalInput").ap())
    shape = arrays["x"].shape
    args.append(nc.dram_tensor("out", shape, F32, kind="ExternalOutput").ap())
    preln_attention_then_routed_ffn(nc, *args)
    return run_bass_kernel_spmd(nc, [arrays], core_ids=[0]).results[0]["out"]
```
